# Optimizing a Trainium2 kernel written in Bass

```python
import numpy as np
import jax
import jax.numpy as jnp

def _softmax(x, axis=-1):
    return jax.nn.softmax(x, axis=axis)

def _gelu(x):
    return jax.nn.gelu(x, approximate=True)

def _silu(x):
    return jax.nn.silu(x)

def _sigmoid(x):
    return jax.nn.sigmoid(x)

def _layernorm(x, axis=-1, eps=1e-05):
    m = jnp.mean(x, axis=axis, keepdims=True)
    v = jnp.var(x, axis=axis, keepdims=True)
    return (x - m) / jnp.sqrt(v + eps)

def _scatter_add(tgt, idx, src, axis=0):
    return tgt.at[idx].add(src)

def _segment_sum(src, seg, n):
    return jax.ops.segment_sum(src, seg, n)
kernel_name = 'mk_dlrm_tower_d1_rec_r8_4e80d6'

def setup_inputs(seed: int=0):
    np.random.seed(seed)
    _w = jnp.asarray

    def _rec_inputs():
        import jax
        import jax.numpy as jnp
        _tk = jax.random.key(seed)
        dense_ctx = jax.random.normal(jax.random.fold_in(_tk, 190), (512, 16), jnp.float32)
        ids = jnp.stack([jax.random.randint(jax.random.fold_in(_tk, 200 + f), (512,), 0, v, jnp.int32) for f, v in enumerate([1000, 125000, 125000, 1250, 12500, 12500, 12500, 1000, 12500, 1000, 1000, 12500, 125000, 1000, 12500, 1250, 125000, 1250, 1000, 1000, 12500, 1000, 1250, 1250, 125000, 1250, 1000, 12500, 1250, 1000, 12500, 1000, 1250, 12500, 125000, 125000, 1250, 1000, 1250])], axis=1)
        tbl_0 = 0.05 * jax.random.normal(jax.random.fold_in(_tk, 500 + 0), (1000, 16), jnp.float32)
        tbl_1 = 0.05 * jax.random.normal(jax.random.fold_in(_tk, 500 + 1), (125000, 16), jnp.float32)
        tbl_2 = 0.05 * jax.random.normal(jax.random.fold_in(_tk, 500 + 2), (125000, 16), jnp.float32)
        tbl_3 = 0.05 * jax.random.normal(jax.random.fold_in(_tk, 500 + 3), (1250, 16), jnp.float32)
        tbl_4 = 0.05 * jax.random.normal(jax.random.fold_in(_tk, 500 + 4), (12500, 16), jnp.float32)
        tbl_5 = 0.05 * jax.random.normal(jax.random.fold_in(_tk, 500 + 5), (12500, 16), jnp.float32)
        tbl_6 = 0.05 * jax.random.normal(jax.random.fold_in(_tk, 500 + 6), (12500, 16), jnp.float32)
        tbl_7 = 0.05 * jax.random.normal(jax.random.fold_in(_tk, 500 + 7), (1000, 16), jnp.float32)
        tbl_8 = 0.05 * jax.random.normal(jax.random.fold_in(_tk, 500 + 8), (12500, 16), jnp.float32)
        tbl_9 = 0.05 * jax.random.normal(jax.random.fold_in(_tk, 500 + 9), (1000, 16), jnp.float32)
        tbl_10 = 0.05 * jax.random.normal(jax.random.fold_in(_tk, 500 + 10), (1000, 16), jnp.float32)
        tbl_11 = 0.05 * jax.random.normal(jax.random.fold_in(_tk, 500 + 11), (12500, 16), jnp.float32)
        tbl_12 = 0.05 * jax.random.normal(jax.random.fold_in(_tk, 500 + 12), (125000, 16), jnp.float32)
        tbl_13 = 0.05 * jax.random.normal(jax.random.fold_in(_tk, 500 + 13), (1000, 16), jnp.float32)
        tbl_14 = 0.05 * jax.random.normal(jax.random.fold_in(_tk, 500 + 14), (12500, 16), jnp.float32)
        tbl_15 = 0.05 * jax.random.normal(jax.random.fold_in(_tk, 500 + 15), (1250, 16), jnp.float32)
        tbl_16 = 0.05 * jax.random.normal(jax.random.fold_in(_tk, 500 + 16), (125000, 16), jnp.float32)
        tbl_17 = 0.05 * jax.random.normal(jax.random.fold_in(_tk, 500 + 17), (1250, 16), jnp.float32)
        tbl_18 = 0.05 * jax.random.normal(jax.random.fold_in(_tk, 500 + 18), (1000, 16), jnp.float32)
        tbl_19 = 0.05 * jax.random.normal(jax.random.fold_in(_tk, 500 + 19), (1000, 16), jnp.float32)
        tbl_20 = 0.05 * jax.random.normal(jax.random.fold_in(_tk, 500 + 20), (12500, 16), jnp.float32)
        tbl_21 = 0.05 * jax.random.normal(jax.random.fold_in(_tk, 500 + 21), (1000, 16), jnp.float32)
        tbl_22 = 0.05 * jax.random.normal(jax.random.fold_in(_tk, 500 + 22), (1250, 16), jnp.float32)
        tbl_23 = 0.05 * jax.random.normal(jax.random.fold_in(_tk, 500 + 23), (1250, 16), jnp.float32)
        tbl_24 = 0.05 * jax.random.normal(jax.random.fold_in(_tk, 500 + 24), (125000, 16), jnp.float32)
        tbl_25 = 0.05 * jax.random.normal(jax.random.fold_in(_tk, 500 + 25), (1250, 16), jnp.float32)
        tbl_26 = 0.05 * jax.random.normal(jax.random.fold_in(_tk, 500 + 26), (1000, 16), jnp.float32)
        tbl_27 = 0.05 * jax.random.normal(jax.random.fold_in(_tk, 500 + 27), (12500, 16), jnp.float32)
        tbl_28 = 0.05 * jax.random.normal(jax.random.fold_in(_tk, 500 + 28), (1250, 16), jnp.float32)
        tbl_29 = 0.05 * jax.random.normal(jax.random.fold_in(_tk, 500 + 29), (1000, 16), jnp.float32)
        tbl_30 = 0.05 * jax.random.normal(jax.random.fold_in(_tk, 500 + 30), (12500, 16), jnp.float32)
        tbl_31 = 0.05 * jax.random.normal(jax.random.fold_in(_tk, 500 + 31), (1000, 16), jnp.float32)
        tbl_32 = 0.05 * jax.random.normal(jax.random.fold_in(_tk, 500 + 32), (1250, 16), jnp.float32)
        tbl_33 = 0.05 * jax.random.normal(jax.random.fold_in(_tk, 500 + 33), (12500, 16), jnp.float32)
        tbl_34 = 0.05 * jax.random.normal(jax.random.fold_in(_tk, 500 + 34), (125000, 16), jnp.float32)
        tbl_35 = 0.05 * jax.random.normal(jax.random.fold_in(_tk, 500 + 35), (125000, 16), jnp.float32)
        tbl_36 = 0.05 * jax.random.normal(jax.random.fold_in(_tk, 500 + 36), (1250, 16), jnp.float32)
        tbl_37 = 0.05 * jax.random.normal(jax.random.fold_in(_tk, 500 + 37), (1000, 16), jnp.float32)
        tbl_38 = 0.05 * jax.random.normal(jax.random.fold_in(_tk, 500 + 38), (1250, 16), jnp.float32)
        _rk = jax.random.fold_in(_tk, 7)
        W_top1 = 0.05 * jax.random.normal(jax.random.fold_in(_tk, 801), (400, 512), jnp.float32)
        W_top2 = 0.0441942 * jax.random.normal(jax.random.fold_in(_tk, 802), (512, 256), jnp.float32)
        W_top3 = 0.0625 * jax.random.normal(jax.random.fold_in(_tk, 803), (256, 1), jnp.float32)
        b_top1 = jnp.zeros((512,), jnp.float32)
        b_top2 = jnp.zeros((256,), jnp.float32)
        return (dense_ctx, ids, tbl_0, tbl_1, tbl_2, tbl_3, tbl_4, tbl_5, tbl_6, tbl_7, tbl_8, tbl_9, tbl_10, tbl_11, tbl_12, tbl_13, tbl_14, tbl_15, tbl_16, tbl_17, tbl_18, tbl_19, tbl_20, tbl_21, tbl_22, tbl_23, tbl_24, tbl_25, tbl_26, tbl_27, tbl_28, tbl_29, tbl_30, tbl_31, tbl_32, tbl_33, tbl_34, tbl_35, tbl_36, tbl_37, tbl_38, W_top1, b_top1, W_top2, b_top2, W_top3)
    dense_ctx, ids, tbl_0, tbl_1, tbl_2, tbl_3, tbl_4, tbl_5, tbl_6, tbl_7, tbl_8, tbl_9, tbl_10, tbl_11, tbl_12, tbl_13, tbl_14, tbl_15, tbl_16, tbl_17, tbl_18, tbl_19, tbl_20, tbl_21, tbl_22, tbl_23, tbl_24, tbl_25, tbl_26, tbl_27, tbl_28, tbl_29, tbl_30, tbl_31, tbl_32, tbl_33, tbl_34, tbl_35, tbl_36, tbl_37, tbl_38, W_top1, b_top1, W_top2, b_top2, W_top3 = _rec_inputs()

    def _L0_rec_setup():
        import jax, jax.numpy as jnp
        import numpy as np
        B, F0, D = (256, 39, 16)
        CROSS = [128, 128, 128]
        key = jax.random.key(seed)
        k0, k1, k2, k3 = jax.random.split(key, 4)
        inputs = jax.random.normal(k0, (B, F0, D), dtype=jnp.float32)
        f0 = jax.random.normal(k1, (F0 * F0, CROSS[0]), dtype=jnp.float32) * 0.05
        f1 = jax.random.normal(k2, (CROSS[0] * F0, CROSS[1]), dtype=jnp.float32) * 0.05
        f2 = jax.random.normal(k3, (CROSS[1] * F0, CROSS[2]), dtype=jnp.float32) * 0.05
        return {'inputs': inputs, 'f0': f0, 'f1': f1, 'f2': f2}
    _L0_rec_all = _L0_rec_setup()
    _L0_rec_in = {k: v for k, v in _L0_rec_all.items() if k in ('f0', 'f1', 'f2')}
    del _L0_rec_all
    return {'dense_ctx': dense_ctx, 'ids': ids, 'tbl_0': tbl_0, 'tbl_1': tbl_1, 'tbl_2': tbl_2, 'tbl_3': tbl_3, 'tbl_4': tbl_4, 'tbl_5': tbl_5, 'tbl_6': tbl_6, 'tbl_7': tbl_7, 'tbl_8': tbl_8, 'tbl_9': tbl_9, 'tbl_10': tbl_10, 'tbl_11': tbl_11, 'tbl_12': tbl_12, 'tbl_13': tbl_13, 'tbl_14': tbl_14, 'tbl_15': tbl_15, 'tbl_16': tbl_16, 'tbl_17': tbl_17, 'tbl_18': tbl_18, 'tbl_19': tbl_19, 'tbl_20': tbl_20, 'tbl_21': tbl_21, 'tbl_22': tbl_22, 'tbl_23': tbl_23, 'tbl_24': tbl_24, 'tbl_25': tbl_25, 'tbl_26': tbl_26, 'tbl_27': tbl_27, 'tbl_28': tbl_28, 'tbl_29': tbl_29, 'tbl_30': tbl_30, 'tbl_31': tbl_31, 'tbl_32': tbl_32, 'tbl_33': tbl_33, 'tbl_34': tbl_34, 'tbl_35': tbl_35, 'tbl_36': tbl_36, 'tbl_37': tbl_37, 'tbl_38': tbl_38, 'W_top1': W_top1, 'b_top1': b_top1, 'W_top2': W_top2, 'b_top2': b_top2, 'W_top3': W_top3, 'L0_rec_f0': _L0_rec_in['f0'], 'L0_rec_f1': _L0_rec_in['f1'], 'L0_rec_f2': _L0_rec_in['f2']}

def reference(dense_ctx, ids, tbl_0, tbl_1, tbl_2, tbl_3, tbl_4, tbl_5, tbl_6, tbl_7, tbl_8, tbl_9, tbl_10, tbl_11, tbl_12, tbl_13, tbl_14, tbl_15, tbl_16, tbl_17, tbl_18, tbl_19, tbl_20, tbl_21, tbl_22, tbl_23, tbl_24, tbl_25, tbl_26, tbl_27, tbl_28, tbl_29, tbl_30, tbl_31, tbl_32, tbl_33, tbl_34, tbl_35, tbl_36, tbl_37, tbl_38, W_top1, b_top1, W_top2, b_top2, W_top3, L0_rec_f0, L0_rec_f1, L0_rec_f2):
    import jax
    import jax.numpy as jnp

    def _L0_rec_ref(inputs, f0, f1, f2):
        import jax, jax.numpy as jnp
        import numpy as np
        B, F0, D = (256, 39, 16)
        CROSS = [128, 128, 128]
        filters = [f0, f1, f2]
        x0 = inputs
        xk = inputs
        outs = []
        for W in filters:
            b, f, d = x0.shape
            g = xk.shape[1]
            z = jnp.einsum('bfd,bgd->bfgd', x0, xk).reshape(b, f * g, d)
            cur = jnp.einsum('bpd,pm->bmd', z, W)
            outs.append(cur)
            xk = cur
        result = jnp.concatenate(outs, axis=1)
        return jnp.sum(result, axis=-1)
    e = jnp.stack([tbl_0[ids[:, 0]], tbl_1[ids[:, 1]], tbl_2[ids[:, 2]], tbl_3[ids[:, 3]], tbl_4[ids[:, 4]], tbl_5[ids[:, 5]], tbl_6[ids[:, 6]], tbl_7[ids[:, 7]], tbl_8[ids[:, 8]], tbl_9[ids[:, 9]], tbl_10[ids[:, 10]], tbl_11[ids[:, 11]], tbl_12[ids[:, 12]], tbl_13[ids[:, 13]], tbl_14[ids[:, 14]], tbl_15[ids[:, 15]], tbl_16[ids[:, 16]], tbl_17[ids[:, 17]], tbl_18[ids[:, 18]], tbl_19[ids[:, 19]], tbl_20[ids[:, 20]], tbl_21[ids[:, 21]], tbl_22[ids[:, 22]], tbl_23[ids[:, 23]], tbl_24[ids[:, 24]], tbl_25[ids[:, 25]], tbl_26[ids[:, 26]], tbl_27[ids[:, 27]], tbl_28[ids[:, 28]], tbl_29[ids[:, 29]], tbl_30[ids[:, 30]], tbl_31[ids[:, 31]], tbl_32[ids[:, 32]], tbl_33[ids[:, 33]], tbl_34[ids[:, 34]], tbl_35[ids[:, 35]], tbl_36[ids[:, 36]], tbl_37[ids[:, 37]], tbl_38[ids[:, 38]]], axis=1)
    z = _L0_rec_ref(e, L0_rec_f0, L0_rec_f1, L0_rec_f2)
    z = z.reshape(z.shape[0], -1)
    h = jnp.concatenate([z, dense_ctx], axis=1)
    h = jnp.maximum(h @ W_top1 + b_top1, 0.0)
    h = jnp.maximum(h @ W_top2 + b_top2, 0.0)
    y = h @ W_top3
    return y

_drawn_inputs = setup_inputs


def setup_inputs(seed=0):
    import zlib

    import numpy as np

    out = dict(_drawn_inputs(seed))
    spreads = {'b_top1': (0.0, 0.637), 'b_top2': (0.0, 0.274)}
    factors = {'tbl_0': 4.38,
     'tbl_1': 4.949,
     'tbl_2': 4.839,
     'tbl_3': 5.078,
     'tbl_4': 5.089,
     'tbl_5': 4.958,
     'tbl_6': 4.819,
     'tbl_7': 4.879,
     'tbl_8': 4.961,
     'tbl_9': 4.271,
     'tbl_10': 5.291,
     'tbl_11': 4.73,
     'tbl_12': 4.423,
     'tbl_13': 4.569,
     'tbl_14': 4.873,
     'tbl_15': 5.032,
     'tbl_16': 5.255,
     'tbl_17': 5.031,
     'tbl_18': 5.426,
     'tbl_19': 4.802,
     'tbl_20': 4.995,
     'tbl_21': 4.836,
     'tbl_22': 4.703,
     'tbl_23': 4.948,
     'tbl_24': 4.545,
     'tbl_25': 4.762,
     'tbl_26': 4.854,
     'tbl_27': 5.199,
     'tbl_28': 4.668,
     'tbl_29': 4.783,
     'tbl_30': 4.79,
     'tbl_31': 4.122,
     'tbl_32': 4.737,
     'tbl_33': 4.986,
     'tbl_34': 4.676,
     'tbl_35': 4.868,
     'tbl_36': 4.697,
     'tbl_37': 5.135,
     'tbl_38': 4.873,
     'L0_rec_f1': 5.002,
     'L0_rec_f2': 8.0}
    for name, (base, spread) in spreads.items():
        noise = np.random.default_rng([zlib.crc32(name.encode()), seed]).standard_normal(out[name].shape)
        drawn = base * np.exp(spread * noise) if base else spread * noise
        out[name] = jnp.asarray(drawn.astype(out[name].dtype))
    for name, factor in factors.items():
        out[name] = (out[name] * factor).astype(out[name].dtype)
    return out
```

```python
from contextlib import ExitStack

import concourse.bass as bass
from concourse import mybir

F32 = mybir.dt.float32
F32R = mybir.dt.float32r
I32 = mybir.dt.int32
ALU = mybir.AluOpType
ACT = mybir.ActivationFunctionType
AX = mybir.AxisListType

B, F, D = 512, 39, 16
M = 128
BB = 32
NBLK = B // BB
COLS = BB * D
TILES = 4
TB = BB // TILES
SHIFTS = (F + 1) // 2
SPT = 3
L0T = -(-SHIFTS // SPT)
ROWS = SPT * F
FPC = 4
CH = -(-F // FPC)
GF = 4
NG = -(-F // GF)
FX = F + 1

PATTERN = ["adaadadaad", "adaadadaad", "adaadadaad", "adaadadaad"]
DIRECT = 2
D_RING, A_RING, P_RING = 2, 3, 4
D_OFF = [sum(p.count("d") for p in PATTERN[:t]) for t in range(TILES + 1)]
A_OFF = [sum(p.count("a") for p in PATTERN[:t]) for t in range(TILES + 1)]
ND, NA = D_OFF[TILES], A_OFF[TILES]
assert ND % D_RING == 0 and NA % A_RING == 0
P_OFF = [A_OFF[t] - DIRECT * t for t in range(TILES + 1)]
NP = P_OFF[TILES]
assert NP % P_RING == 0
ADD_OFF = [P_OFF[t] - t for t in range(TILES + 1)]
NADD = ADD_OFF[TILES]
EARLY_Z0 = 2
Z0_AT = [(0, 1), (0, 2), (0, 3), (1, 1), (1, 2)]
L0_AT = {0: {6: [0], 8: [1]}, 1: {0: [2], 2: [3], 4: [4], 6: [5], 8: [6]}}
GATHERS_AT = [0, 4, 3, 3]
LAST = BB * (F - FPC * (CH - 1))
assert BB * FPC == 128 and SHIFTS % FPC == 0
SCR_DMAS, LOAD_DMAS = 3, 4
W2_EARLY = 28


def adds_before_free(p):
    t = max(t for t in range(TILES) if P_OFF[t] <= p)
    return ADD_OFF[t] + max(p - P_OFF[t], 1)


def starts(b):
    return isinstance(b, int) and b == 0


def build(nc, tables, ids, base, w0a, w0b, w1, w2, wt1, bt1, wt2, bt2, wt3, dense, mask, ident, out):
    scratch = nc.dram_tensor("x0_rows", (F + SHIFTS, BB, D), F32, kind="Internal").ap()
    scr_rows = scratch.rearrange("f b d -> f (b d)")
    H1T, H2T = wt1.shape[1] // 128, wt2.shape[1] // 128

    with ExitStack() as ctx:
        def sb(name, shape, dt=F32):
            return ctx.enter_context(nc.sbuf_tensor(name, shape, dt))

        def sem(name):
            return ctx.enter_context(nc.semaphore(name))

        w1h = sb("w1h", [128, F * M], F32R)
        w1l = sb("w1l", [128, F * M], F32R)
        w0s = sb("w0s", [128, L0T, M])
        w2late = sb("w2late", [128, (F - W2_EARLY) * M])
        wt1_sb = sb("wt1_sb", [128, 4, H1T * 128])
        wt2_sb = sb("wt2_sb", [128, H1T, H2T * 128])
        wt3_sb = sb("wt3_sb", [128, H2T])
        bt1_sb = sb("bt1_sb", [128, H1T])
        bt2_sb = sb("bt2_sb", [128, H2T])
        mask_sb = sb("mask_sb", [128, TB])
        ident_sb = sb("ident_sb", [128, ROWS])
        dense_sb = sb("dense_sb", [16, B])
        ids_sb = sb("ids_sb", [128, NBLK * CH], I32)
        base_sb = sb("base_sb", [128, CH], I32)
        idx = sb("idx", [128, CH], I32)
        emb = sb("emb", [128, CH, D])
        x0t = sb("x0t", [128, COLS])
        pairs = sb("pairs", [128, L0T, COLS])
        x1f = sb("x1f", [128, COLS])
        x1h = sb("x1h", [128, COLS], F32R)
        x1l = sb("x1l", [128, COLS], F32R)
        x0c = sb("x0c", [128, TILES, FX])
        prods = sb("prods", [128, P_RING, GF * M])
        parts = sb("parts", [128, 2, 2 + DIRECT, GF * M])
        cur1 = sb("cur1", [128, 2, M])
        x0d = sb("x0d", [128, 2, TB, FX])
        gram = sb("gram", [128, FX, B])
        s0 = sb("s0", [128, B])
        s2 = sb("s2", [128, B])
        y_sb = sb("y_sb", [1, B])
        graw = gram[:, :, :].rearrange("p f b -> p (f b)")
        w1raw = graw[:, 0:F * M]
        w0braw = graw[:, F * M:F * M + L0T * M].rearrange("p (t m) -> p t m", m=M)
        w2early = pairs[:, :, :].rearrange("p t n -> p (t n)")
        h1 = prods[:, 0:H1T, :]
        h2 = parts[:, 0, 0:H2T, :]

        psd = [ctx.enter_context(nc.psum_tensor(f"psd{i}", [128, 512], F32)) for i in range(D_RING)]
        psa = [ctx.enter_context(nc.psum_tensor(f"psa{i}", [128, 512], F32)) for i in range(A_RING)]
        ps0 = ctx.enter_context(nc.psum_tensor("ps0", [128, 512], F32))
        pst = ctx.enter_context(nc.psum_tensor("pst", [128, 512], F32))
        psg = ctx.enter_context(nc.psum_tensor("psg", [128, 512], F32))

        ids_in, w0_in, w1_in, const_in, mlp_in, w2a_in, w2b_in = (
            sem(n) for n in ("ids_in", "w0_in", "w1_in", "const_in", "mlp_in", "w2a_in", "w2b_in"))
        w0_summed = sem("w0_summed")
        w1h_ready = sem("w1h_ready")
        w1l_ready = sem("w1l_ready")
        ones_ready = sem("ones_ready")
        idx_ready = sem("idx_ready")
        gathered = sem("gathered")
        scr_written = sem("scr_written")
        loaded = sem("loaded")
        z0_ready = sem("z0_ready")
        l0_done = sem("l0_done")
        tr_done = sem("tr_done")
        x1f_ready = sem("x1f_ready")
        x1h_ready = sem("x1h_ready")
        x1l_ready = sem("x1l_ready")
        x0c_ready = sem("x0c_ready")
        y_d = sem("y_d")
        y_a = sem("y_a")
        acc_steps = sem("acc_steps")
        act_prods = sem("act_prods")
        pool_adds = sem("pool_adds")
        c1_ready = sem("c1_ready")
        x0d_ready = sem("x0d_ready")
        g2_done = sem("g2_done")
        g2_copied = sem("g2_copied")
        l2_done = sem("l2_done")
        s2_ready = sem("s2_ready")
        h1_done = sem("h1_done")
        h1_ready = sem("h1_ready")
        h2_done = sem("h2_done")
        h2_ready = sem("h2_ready")
        y_done = sem("y_done")
        y_ready = sem("y_ready")
        stored = sem("stored")

        block = ctx.enter_context(nc.Block())

        @block.sync
        def _(sp):
            def rows_at(row, parts, n):
                return bass.AP(scr_rows.tensor, row * COLS, [[D, parts], [FPC * COLS, n], [1, D]])

            def rows_to_dram(b):
                sp.wait_ge(gathered, 16 * CH * (b + 1))
                if not starts(b):
                    sp.wait_ge(loaded, 16 * LOAD_DMAS * b)
                sp.dma_start(rows_at(0, 128, CH - 1), emb[:, 0:CH - 1, :]).then_inc(scr_written, 16)
                sp.dma_start(rows_at(FPC * (CH - 1), LAST, 1), emb[0:LAST, CH - 1:CH, :]).then_inc(scr_written, 16)
                sp.dma_start(rows_at(F, 128, SHIFTS // FPC), emb[:, 0:SHIFTS // FPC, :]).then_inc(scr_written, 16)

            def load_rows(b):
                sp.wait_ge(scr_written, 16 * SCR_DMAS * (b + 1))
                if not starts(b):
                    sp.wait_ge(l0_done, b)
                    sp.wait_ge(tr_done, b)
                src = bass.AP(scr_rows.tensor, 0, [[0, SPT], [COLS, F], [1, COLS]])
                sp.dma_start(x0t[0:ROWS, :], src).then_inc(loaded, 16)
                for k in range(SPT):
                    n = len(range(k, SHIFTS, SPT))
                    src = bass.AP(scr_rows.tensor, k * COLS, [[COLS, F], [SPT * COLS, n], [1, COLS]])
                    sp.dma_start(pairs[F * k:F * k + F, 0:n, :], src).then_inc(loaded, 16)

            sp.dma_start(ids_sb[:, :], ids).then_inc(ids_in, 16)
            sp.dma_start(base_sb[:, :], base).then_inc(ids_in, 16)
            sp.dma_start(w0s[0:ROWS, :, :], w0a).then_inc(w0_in, 16)
            sp.dma_start(w0braw[F:ROWS, 0, :], w0b[F:ROWS, 0, :]).then_inc(w0_in, 16)
            sp.dma_start(w0braw[0:ROWS, 1:L0T, :], w0b[:, 1:L0T, :]).then_inc(w0_in, 16)
            sp.dma_start(w1raw.rearrange("g (f m) -> g f m", m=M), w1.rearrange("(f g) m -> g f m", g=128)).then_inc(w1_in, 16)
            rows_to_dram(0)
            load_rows(0)
            rows_to_dram(1)
            load_rows(1)
            rows_to_dram(2)
            load_rows(2)
            with sp.Fori(1, NBLK - 2) as b:
                rows_to_dram(b + 2)
                load_rows(b + 2)
            w2v = w2.rearrange("(f g) m -> g f m", g=128)
            sp.dma_start(w2late[:, :].rearrange("g (f m) -> g f m", m=M), w2v[:, W2_EARLY:F, :]).then_inc(w2b_in, 16)
            sp.dma_start(wt1_sb[:, 0:3, :], wt1[0:384, :].rearrange("(k p) n -> p k n", p=128)).then_inc(mlp_in, 16)
            sp.dma_start(wt1_sb[0:16, 3, :], wt1[384:400, :]).then_inc(mlp_in, 16)
            sp.dma_start(wt2_sb[:, :, :], wt2.rearrange("(k p) n -> p k n", p=128)).then_inc(mlp_in, 16)
            sp.wait_ge(l0_done, NBLK)
            sp.dma_start(w2early.rearrange("g (f m) -> g f m", m=M), w2v[:, 0:W2_EARLY, :]).then_inc(w2a_in, 16)
            sp.wait_ge(y_ready, 1)
            sp.dma_start(out.rearrange("b o -> o b"), y_sb[:, :]).then_inc(stored, 16)
            sp.wait_ge(stored, 16)

        @block.gpsimd
        def _(pool):
            def row_numbers(b, at):
                if not starts(b):
                    pool.wait_ge(scr_written, 16 * SCR_DMAS * b)
                pool.tensor_tensor(idx[:, :], ids_sb[:, at], base_sb[:, :], ALU.add).then_inc(idx_ready, 1)

            def gather(c):
                n = BB * min(FPC, F - FPC * c)
                pool.indirect_dma_start(emb[0:n, c, :], None, tables,
                                        bass.IndirectOffsetOnAxis(idx[0:n, c:c + 1], 0)).then_inc(gathered, 16)

            def block_of(b, gather_ahead, at=None):
                c = 0
                for t in range(TILES):
                    T = b * TILES + t
                    n_adds = ADD_OFF[t + 1] - ADD_OFF[t]
                    for k in range(max(n_adds, GATHERS_AT[t])):
                        if gather_ahead and t == 0 and k == n_adds - 1:
                            row_numbers(b + 3, at)
                        if k == 1:
                            pool.wait_ge(x0c_ready, T + 1)
                            if t >= 2 or not starts(b):
                                pool.wait_ge(g2_done, T - 1)
                            pool.tensor_tensor(x0d[:, t % 2, :, :],
                                               x0c[:, t, :].unsqueeze(1).to_broadcast([128, TB, FX]),
                                               mask_sb[:, :].unsqueeze(2).to_broadcast([128, TB, FX]),
                                               ALU.mult).then_inc(x0d_ready, 1)
                        if k < n_adds:
                            p = P_OFF[t] + k + 1
                            if k == 0:
                                if t >= 2 or not starts(b):
                                    pool.wait_ge(c1_ready, T - 1)
                            else:
                                pool.wait_ge(pool_adds, b * NADD + ADD_OFF[t] + k)
                            pool.wait_ge(act_prods, b * NA + A_OFF[t] + k + 2)
                            first = prods[:, (p - 1) % P_RING, :] if k == 0 else parts[:, t % 2, 1, :]
                            if gather_ahead and t == 1 and k == 0:
                                pool.wait_ge(idx_ready, b + 4)
                            pool.tensor_tensor(parts[:, t % 2, 1, :], first, prods[:, p % P_RING, :],
                                               ALU.add).then_inc(pool_adds, 1)
                        if gather_ahead and k < GATHERS_AT[t]:
                            gather(c)
                            c += 1

            pool.wait_ge(ids_in, 32)
            for b in range(3):
                row_numbers(b, slice(b * CH, b * CH + CH))
                pool.wait_ge(idx_ready, b + 1)
                for c in range(CH):
                    gather(c)
                if b == 0:
                    pool.memset(x0c[:, :, F:FX], 1.0).then_inc(ones_ready, 1)
            pool.wait_ge(ones_ready, 1)
            pool.wait_ge(const_in, 16 * 5)
            block_of(0, True, slice(3 * CH, 4 * CH))
            with pool.Fori(1, NBLK - 3) as b:
                block_of(b, True, bass.ds((b + 3) * CH, CH))
            block_of(NBLK - 3, False)
            block_of(NBLK - 2, False)
            block_of(NBLK - 1, False)

        @block.vector
        def _(dve):
            def z0(b, k):
                if k == 0:
                    dve.wait_ge(loaded, 16 * LOAD_DMAS * (b + 1))
                rows = F * len(range(SPT * k, min(SPT * k + SPT, SHIFTS)))
                dve.tensor_tensor(pairs[0:rows, k, :], x0t[0:rows, :], pairs[0:rows, k, :], ALU.mult).then_inc(z0_ready, 1)

            def low_part(b, t):
                dve.wait_ge(x1h_ready, b * TILES + t + 1)
                c = slice(128 * t, 128 * t + 128)
                dve.tensor_tensor(x1l[:, c], x1f[:, c], x1h[:, c].bitcast(F32), ALU.subtract).then_inc(x1l_ready, 1)

            def sum_cur0(b, at):
                dve.wait_ge(x1f_ready, b + 1)
                dve.tensor_reduce(s0[:, at], x1f[:, :].rearrange("p (b d) -> p b d", d=D), AX.X, ALU.add)

            def finish_tile(T, t):
                if not isinstance(T, int) or T >= 2:
                    dve.wait_ge(g2_done, T - 1)
                dve.tensor_reduce(cur1[:, t % 2, :],
                                  parts[:, t % 2, :, :].rearrange("p k (j m) -> p m (k j)", m=M),
                                  AX.X, ALU.add).then_inc(c1_ready, 1)

            def block_of(b, ahead, ahead2, at=None):
                for t in range(TILES):
                    T = b * TILES + t
                    groups = [g for g in range(NG) if PATTERN[t][g] == "d"]
                    for n, g in enumerate(groups):
                        d = D_OFF[t] + n
                        y = psd[d % D_RING]
                        G = b * ND + d
                        dve.wait_ge(y_d, G + 1)
                        if n == 0:
                            dve.wait_ge(x0c_ready, T + 1)
                            dve.tensor_tensor(parts[:, t % 2, 0, :].rearrange("p (j m) -> p j m", m=M),
                                              y[:, :].rearrange("p (j m) -> p j m", m=M),
                                              x0c[:, t, GF * g:GF * g + GF].unsqueeze(2).to_broadcast([128, GF, M]),
                                              ALU.mult).then_inc(acc_steps, 2)
                        else:
                            nf = min(GF, F - GF * g)
                            for j in range(nf):
                                if j == 0:
                                    dve.wait_ge(acc_steps, 2 * G - 1)
                                if j == 2:
                                    dve.wait_ge(acc_steps, 2 * G)
                                acc = parts[:, t % 2, 0, M * j:M * j + M]
                                op = dve.scalar_tensor_tensor(acc, y[:, M * j:M * j + M],
                                                              x0c[:, t, GF * g + j:GF * g + j + 1], acc,
                                                              ALU.mult, ALU.add)
                                if j in (1, nf - 1):
                                    op.then_inc(acc_steps, 1)
                        if n == 0:
                            tp = (t - 1) % TILES
                            bp = b if t else b - 1
                            if t or not starts(b):
                                dve.wait_ge(act_prods, bp * NA + A_OFF[tp + 1])
                                dve.wait_ge(pool_adds, bp * NADD + ADD_OFF[tp + 1])
                                dve.wait_ge(acc_steps, 2 * (bp * ND + D_OFF[tp + 1]))
                                finish_tile(T - 1, tp)
                        if t == 1 and n == 3:
                            low_part(b, TILES - 1)
                        if ahead and (t, n) in Z0_AT:
                            z0(b + 1, EARLY_Z0 + Z0_AT.index((t, n)))
                        if t == 2 and ahead and n == 2:
                            sum_cur0(b + 1, at)
                        if t == 2 and ahead and n == 3:
                            low_part(b + 1, 0)
                            low_part(b + 1, 1)
                        if t == 3 and ahead and n == 1:
                            low_part(b + 1, 2)
                        if ahead2 and t == 3 and 0 < n <= EARLY_Z0:
                            z0(b + 2, n - 1)

            dve.memset(w0braw[0:F, 0, :], 0.0).then_inc(w0_summed, 1)
            dve.wait_ge(w0_summed, 1)
            dve.wait_ge(w0_in, 48)
            dve.tensor_tensor(w0s[0:ROWS, :, :], w0s[0:ROWS, :, :], w0braw[0:ROWS, :, :], ALU.add).then_inc(w0_summed, 1)
            third = F * M // 3
            for k in range(3):
                c = slice(k * third, (k + 1) * third)
                dve.wait_ge(w1h_ready, k + 1)
                dve.tensor_tensor(w1l[:, c], w1raw[:, c], w1h[:, c].bitcast(F32), ALU.subtract).then_inc(w1l_ready, 1)
            for k in range(L0T):
                z0(0, k)
            sum_cur0(0, slice(0, BB))
            for t in range(3):
                low_part(0, t)
            for k in range(EARLY_Z0):
                z0(1, k)
            block_of(0, True, True, slice(BB, 2 * BB))
            with dve.Fori(1, NBLK - 2) as b:
                block_of(b, True, True, bass.ds((b + 1) * BB, BB))
            block_of(NBLK - 2, True, False, slice((NBLK - 1) * BB, NBLK * BB))
            block_of(NBLK - 1, False, False)
            dve.wait_ge(act_prods, NBLK * NA)
            dve.wait_ge(pool_adds, NBLK * NADD)
            dve.wait_ge(acc_steps, 2 * NBLK * ND)
            finish_tile(NBLK * TILES - 1, TILES - 1)

        @block.scalar
        def _(act):
            def load_cur0(b):
                act.wait_ge(l0_done, b + 1)
                if not starts(b):
                    act.wait_ge(x1l_ready, b * TILES)
                act.activation(x1f[:, :], ps0[:, :], ACT.Copy).then_inc(x1f_ready, 1)
                act.wait_ge(x1f_ready, b + 1)

            def high_part(b, t):
                c = slice(128 * t, 128 * t + 128)
                if not starts(b):
                    act.wait_ge(y_d, (b - 1) * ND + D_OFF[t + 1])
                act.activation(x1h[:, c], x1f[:, c], ACT.Copy).then_inc(x1h_ready, 1)

            def scalars(b, t):
                act.wait_ge(tr_done, b + 1)
                if not starts(b):
                    act.wait_ge(acc_steps, 2 * ((b - 1) * ND + D_OFF[t + 1]))
                    act.wait_ge(x0d_ready, (b - 1) * TILES + t + 1)
                act.activation(x0c[:, t, 0:F], pst[:, ROWS * t:ROWS * t + F], ACT.Copy).then_inc(x0c_ready, 1)

            def gram_out(T, at):
                act.wait_ge(g2_done, T + 1)
                act.activation(gram[:, :, at], psg[:, 0:TB * FX].rearrange("p (b f) -> p f b", f=FX),
                               ACT.Copy).then_inc(g2_copied, 1)

            def block_of(b, ahead):
                for t in range(TILES):
                    T = b * TILES + t
                    groups = [g for g in range(NG) if PATTERN[t][g] == "a"]
                    for n, g in enumerate(groups):
                        a = A_OFF[t] + n
                        y = psa[a % A_RING]
                        act.wait_ge(y_a, b * NA + a + 1)
                        if n == 0:
                            act.wait_ge(x0c_ready, T + 1)
                        if n < len(groups) - DIRECT:
                            p = P_OFF[t] + n
                            dst = prods[:, p % P_RING, :]
                            if p >= P_RING:
                                act.wait_ge(pool_adds, b * NADD + adds_before_free(p - P_RING))
                            elif not starts(b):
                                act.wait_ge(pool_adds, (b - 1) * NADD + adds_before_free(p - P_RING + NP))
                        else:
                            dst = parts[:, t % 2, 2 + n - (len(groups) - DIRECT), :]
                            if t >= 2 or not starts(b):
                                act.wait_ge(c1_ready, T - 1)
                        for j in range(GF):
                            op = act.activation(dst[:, M * j:M * j + M], y[:, M * j:M * j + M], ACT.Copy,
                                                scale=x0c[:, t, GF * g + j:GF * g + j + 1])
                        op.then_inc(act_prods, 1)
                        if n == 1 and (t >= 2 or not starts(b)):
                            at = (slice((T - 2) * TB, (T - 1) * TB) if isinstance(T, int)
                                  else bass.ds((T - 2) * TB, TB))
                            gram_out(T - 2, at)
                        if t == 0 and n == 0:
                            high_part(b, 3)
                        if t == 0 and n == 2:
                            scalars(b, 3)
                        if t == 2 and ahead:
                            if n == 2:
                                load_cur0(b + 1)
                            if n == 3:
                                high_part(b + 1, 0)
                                scalars(b + 1, 0)
                            if n == 4:
                                high_part(b + 1, 1)
                            if n == 5:
                                scalars(b + 1, 1)
                        if t == 3 and ahead:
                            if n == 2:
                                high_part(b + 1, 2)
                            if n == 3:
                                scalars(b + 1, 2)

            act.dma_start(ident_sb[0:ROWS, :], ident).then_inc(const_in, 16)
            act.dma_start(mask_sb[:, :], mask).then_inc(const_in, 16)
            act.dma_start(bt1_sb[:, :], bt1).then_inc(const_in, 16)
            act.dma_start(bt2_sb[:, :], bt2).then_inc(const_in, 16)
            act.dma_start(wt3_sb[:, :], wt3).then_inc(const_in, 16)
            act.dma_start(dense_sb[:, :], dense).then_inc(mlp_in, 16)
            act.wait_ge(w1_in, 16)
            third = F * M // 3
            for k in range(3):
                c = slice(k * third, (k + 1) * third)
                act.activation(w1h[:, c], w1raw[:, c], ACT.Copy).then_inc(w1h_ready, 1)
            load_cur0(0)
            for t in range(3):
                high_part(0, t)
            act.wait_ge(w1l_ready, 3)
            for t in range(3):
                scalars(0, t)
            block_of(0, True)
            with act.Fori(1, NBLK - 2) as b:
                block_of(b, True)
            block_of(NBLK - 2, True)
            block_of(NBLK - 1, False)
            for T in range(NBLK * TILES - 2, NBLK * TILES):
                gram_out(T, slice(T * TB, (T + 1) * TB))
            act.wait_ge(l2_done, 1)
            act.activation(s2[:, :], psg[:, :], ACT.Copy).then_inc(s2_ready, 1)
            act.wait_ge(const_in, 16 * 5)
            act.wait_ge(pool_adds, NBLK * NADD)
            for m, y in enumerate([ps0, pst, psa[0], psa[1]][:H1T]):
                act.wait_ge(h1_done, m + 1)
                act.activation(h1[:, m, :], y[:, :], ACT.Relu, bias=bt1_sb[:, m:m + 1]).then_inc(h1_ready, 1)
            for m in range(H2T):
                act.wait_ge(h2_done, m + 1)
                act.activation(h2[:, m, :], psd[m][:, :], ACT.Relu, bias=bt2_sb[:, m:m + 1]).then_inc(h2_ready, 1)
            act.wait_ge(y_done, 1)
            act.activation(y_sb[:, :], psg[0:1, :], ACT.Copy).then_inc(y_ready, 1)

        @block.tensor
        def _(pe):
            def layer0(b, k):
                if k == 0 and not starts(b):
                    pe.wait_ge(x1f_ready, b)
                pe.wait_ge(z0_ready, b * L0T + k + 1)
                rows = F * len(range(SPT * k, min(SPT * k + SPT, SHIFTS)))
                op = pe.matmul(ps0[:, :], w0s[0:rows, k, :], pairs[0:rows, k, :], start=(k == 0), stop=(k == L0T - 1))
                if k == L0T - 1:
                    op.then_inc(l0_done, 1)

            def turn_x0(b):
                pe.wait_ge(loaded, 16 * LOAD_DMAS * (b + 1))
                if not starts(b):
                    pe.wait_ge(x0c_ready, b * TILES)
                for t in range(TILES):
                    op = pe.transpose(pst[:, ROWS * t:ROWS * t + ROWS], x0t[0:ROWS, 128 * t:128 * t + 128], ident_sb[0:ROWS, :])
                op.then_inc(tr_done, 1)

            def grams(T, t):
                pe.wait_ge(c1_ready, T + 1)
                pe.wait_ge(x0d_ready, T + 1)
                if not isinstance(T, int) or T > 0:
                    pe.wait_ge(g2_copied, T)
                pe.matmul(psg[:, 0:TB * FX], cur1[:, t % 2, :], x0d[:, t % 2, :, :].rearrange("p b f -> p (b f)"),
                          start=True, stop=True).then_inc(g2_done, 1)

            def block_of(b, ahead):
                for t in range(TILES):
                    T = b * TILES + t
                    d, a = D_OFF[t], A_OFF[t]
                    hi, lo = x1h[:, 128 * t:128 * t + 128], x1l[:, 128 * t:128 * t + 128]
                    pe.wait_ge(x1h_ready, T + 1)
                    pe.wait_ge(x1l_ready, T + 1)
                    for g in range(NG):
                        n = M * min(GF, F - GF * g)
                        c = slice(GF * M * g, GF * M * g + n)
                        if PATTERN[t][g] == "d":
                            y, full = psd[d % D_RING], y_d
                            if d >= D_RING or not starts(b):
                                pe.wait_ge(acc_steps, 2 * (b * ND + d - D_RING + 1))
                            d += 1
                        else:
                            y, full = psa[a % A_RING], y_a
                            if a >= A_RING or not starts(b):
                                pe.wait_ge(act_prods, b * NA + a - A_RING + 1)
                            a += 1
                        pe.matmul(y[:, 0:n], hi, w1h[:, c], start=True, stop=False)
                        pe.matmul(y[:, 0:n], hi, w1l[:, c], start=False, stop=False)
                        pe.matmul(y[:, 0:n], lo, w1h[:, c], start=False, stop=True).then_inc(full, 1)
                        if ahead:
                            for k in L0_AT.get(t, {}).get(g, []):
                                layer0(b + 1, k)
                            if t == 1 and g == 5:
                                turn_x0(b + 1)
                        if g == NG - 1 and (t or not starts(b)):
                            grams(T - 1, (t - 1) % TILES)

            pe.wait_ge(w0_summed, 2)
            pe.wait_ge(const_in, 16 * 5)
            for k in range(L0T):
                layer0(0, k)
            turn_x0(0)
            pe.wait_ge(w1h_ready, 3)
            pe.wait_ge(w1l_ready, 3)
            block_of(0, True)
            with pe.Fori(1, NBLK - 2) as b:
                block_of(b, True)
            block_of(NBLK - 2, True)
            block_of(NBLK - 1, False)
            grams(NBLK * TILES - 1, TILES - 1)

            pe.wait_ge(w2a_in, 16)
            pe.wait_ge(w2b_in, 16)
            pe.wait_ge(g2_copied, NBLK * TILES)
            for f in range(F):
                w = w2early[:, M * f:M * f + M] if f < W2_EARLY else w2late[:, M * (f - W2_EARLY):M * (f - W2_EARLY) + M]
                op = pe.matmul(psg[:, :], w, gram[:, f, :], start=(f == 0), stop=(f == F - 1))
            op.then_inc(l2_done, 1)

            pe.wait_ge(mlp_in, 16 * 4)
            banks = [ps0, pst, psa[0], psa[1]][:H1T]
            for m, y in enumerate(banks):
                c = slice(128 * m, 128 * m + 128)
                pe.matmul(y[:, :], wt1_sb[:, 0, c], s0[:, :], start=True, stop=False)
                pe.matmul(y[:, :], wt1_sb[:, 1, c], gram[:, F, :], start=False, stop=False)
                pe.matmul(y[:, :], wt1_sb[0:16, 3, c], dense_sb[:, :], start=False, stop=False)
            pe.wait_ge(s2_ready, 1)
            for m, y in enumerate(banks):
                c = slice(128 * m, 128 * m + 128)
                pe.matmul(y[:, :], wt1_sb[:, 2, c], s2[:, :], start=False, stop=True).then_inc(h1_done, 1)
            for k in range(H1T):
                pe.wait_ge(h1_ready, k + 1)
                for m in range(H2T):
                    op = pe.matmul(psd[m][:, :], wt2_sb[:, k, 128 * m:128 * m + 128], h1[:, k, :],
                                   start=(k == 0), stop=(k == H1T - 1))
                    if k == H1T - 1:
                        op.then_inc(h2_done, 1)
            for k in range(H2T):
                pe.wait_ge(h2_ready, k + 1)
                op = pe.matmul(psg[0:1, :], wt3_sb[:, k:k + 1], h2[:, k, :], start=(k == 0), stop=(k == H2T - 1))
            op.then_inc(y_done, 1)


def kernel(**inputs):
    import numpy as np
    import concourse.bacc as bacc
    from concourse.bass_utils import run_bass_kernel_spmd

    nc = bacc.Bacc("TRN2", target_bir_lowering=False, num_devices=1)
    arr = {k: np.asarray(v) for k, v in inputs.items()}
    tabs = [arr[f"tbl_{f}"] for f in range(F)]
    start = np.concatenate([[0], np.cumsum([t.shape[0] for t in tabs])])[:F]

    ids = np.concatenate([arr["ids"], arr["ids"][:, 0:CH * FPC - F]], axis=1)
    ids = ids.reshape(NBLK, BB, CH, FPC).transpose(3, 1, 0, 2).reshape(128, NBLK * CH)
    first_row = np.zeros(CH * FPC, np.int32)
    first_row[:F] = start
    base = np.repeat(first_row.reshape(CH, FPC).T, BB, axis=0)

    f_of = np.arange(SPT * L0T * F).reshape(SPT * L0T, F) % F
    g_of = (f_of + np.arange(SPT * L0T)[:, None]) % F
    w0 = arr["L0_rec_f0"]

    def by_tile(rows):
        return np.ascontiguousarray(w0[rows.reshape(-1)].reshape(L0T, ROWS, M).transpose(1, 0, 2))

    samples = np.arange(128)[:, None] // D == np.arange(TB)[None, :]
    arrays = {
        "tables": np.concatenate(tabs, axis=0),
        "ids_by_block": np.ascontiguousarray(ids),
        "first_rows": np.ascontiguousarray(base.astype(np.int32)),
        "w0_pairs": by_tile(f_of * F + g_of),
        "w0_mirrored": by_tile(g_of * F + f_of),
        "w1": arr["L0_rec_f1"],
        "w2": arr["L0_rec_f2"],
        "w_top1": arr["W_top1"],
        "b_top1": np.ascontiguousarray(arr["b_top1"].reshape(-1, 128).T),
        "w_top2": arr["W_top2"],
        "b_top2": np.ascontiguousarray(arr["b_top2"].reshape(-1, 128).T),
        "w_top3": np.ascontiguousarray(arr["W_top3"].reshape(-1, 128).T),
        "dense": np.ascontiguousarray(arr["dense_ctx"].T),
        "sample_mask": samples.astype(np.float32),
        "identity": np.eye(ROWS, dtype=np.float32),
    }
    args = [nc.dram_tensor(k, v.shape, mybir.dt.from_np(v.dtype), kind="ExternalInput").ap() for k, v in arrays.items()]
    out = nc.dram_tensor("out_0", (B, 1), F32, kind="ExternalOutput").ap()
    build(nc, *args, out)
    result = run_bass_kernel_spmd(nc, [arrays], core_ids=[0])
    return result.results[0]["out_0"]
```

```python
from contextlib import ExitStack

import concourse.bass as bass
from concourse import mybir

F32 = mybir.dt.float32
F32R = mybir.dt.float32r
I32 = mybir.dt.int32
ALU = mybir.AluOpType
ACT = mybir.ActivationFunctionType
AX = mybir.AxisListType

B, F, D = 512, 39, 16
M = 128
BB = 32
NBLK = B // BB
COLS = BB * D
TILES = 4
TB = BB // TILES
SHIFTS = (F + 1) // 2
SPT = 3
L0T = -(-SHIFTS // SPT)
ROWS = SPT * F
FPC = 4
CH = -(-F // FPC)
GF = 4
NG = -(-F // GF)
FX = F + 1

PATTERN = ["adaadadaad", "adaadadaad", "adaadadaad", "adaadadaad"]
DIRECT = 2
D_RING, A_RING, P_RING = 2, 3, 4
D_OFF = [sum(p.count("d") for p in PATTERN[:t]) for t in range(TILES + 1)]
A_OFF = [sum(p.count("a") for p in PATTERN[:t]) for t in range(TILES + 1)]
ND, NA = D_OFF[TILES], A_OFF[TILES]
assert ND % D_RING == 0 and NA % A_RING == 0
P_OFF = [A_OFF[t] - DIRECT * t for t in range(TILES + 1)]
NP = P_OFF[TILES]
assert NP % P_RING == 0
ADD_OFF = [P_OFF[t] - t for t in range(TILES + 1)]
NADD = ADD_OFF[TILES]
EARLY_Z0 = 2
Z0_AT = {(0, 1): 2, (0, 2): 3, (0, 3): 4, (1, 1): 5, (1, 2): 6}
L0_AT = {(0, 6): 0, (0, 8): 1, (1, 0): 2, (1, 2): 3, (1, 4): 4, (1, 6): 5, (1, 8): 6}
Z0_AT_FIRST = {(0, 2): 0, (0, 3): 1, (1, 0): 2, (1, 1): 3, (1, 2): 4, (1, 3): 5, (2, 0): 6}
L0_AT_FIRST = {(1, 0): 0, (1, 2): 1, (1, 5): 2, (1, 6): 3, (1, 8): 4, (2, 0): 5, (2, 1): 6}
FIRST_PIECES = [(0, 1), (1, 3), (3, L0T)]
GATHERS_AT = [0, 4, 3, 3]
LAST = BB * (F - FPC * (CH - 1))
assert BB * FPC == 128 and SHIFTS % FPC == 0
SCR_DMAS, LOAD_DMAS = 3, 4
W2_EARLY = 28
W2_CHUNK, W2_RING = 7, 3
W2_CHUNKS = [(f, min(f + W2_CHUNK, F)) for f in range(0, F, W2_CHUNK)]
L2_RING = 4
assert W2_EARLY % W2_CHUNK == 0 and W2_RING * W2_CHUNK * M + L2_RING * B <= F * M


def on_pool(f):
    return f % 4 == 3


def turn(f, pool):
    return sum(on_pool(i) == pool for i in range(f + 1))


def adds_before_free(p):
    t = max(t for t in range(TILES) if P_OFF[t] <= p)
    return ADD_OFF[t] + max(p - P_OFF[t], 1)


def starts(b):
    return isinstance(b, int) and b == 0


def build(nc, tables, ids, base, w0a, w0b, w1, w2, wt1, bt1, wt2, bt2, wt3, dense, mask, ident, out):
    scratch = nc.dram_tensor("x0_rows", (F + SHIFTS, BB, D), F32, kind="Internal").ap()
    scr_rows = scratch.rearrange("f b d -> f (b d)")
    H1T, H2T = wt1.shape[1] // 128, wt2.shape[1] // 128

    with ExitStack() as ctx:
        def sb(name, shape, dt=F32):
            return ctx.enter_context(nc.sbuf_tensor(name, shape, dt))

        def sem(name):
            return ctx.enter_context(nc.semaphore(name))

        w1h = sb("w1h", [128, F * M], F32R)
        w1l = sb("w1l", [128, F * M], F32R)
        w0s = sb("w0s", [128, L0T, M])
        w2late = sb("w2late", [128, (F - W2_EARLY) * M])
        wt1_sb = sb("wt1_sb", [128, 4, H1T * 128])
        wt2_sb = sb("wt2_sb", [128, H1T, H2T * 128])
        wt3_sb = sb("wt3_sb", [128, H2T])
        bt1_sb = sb("bt1_sb", [128, H1T])
        bt2_sb = sb("bt2_sb", [128, H2T])
        mask_sb = sb("mask_sb", [128, TB])
        ident_sb = sb("ident_sb", [128, ROWS])
        dense_sb = sb("dense_sb", [16, B])
        ids_sb = sb("ids_sb", [128, NBLK * CH], I32)
        base_sb = sb("base_sb", [128, CH], I32)
        idx = sb("idx", [128, CH], I32)
        idx_first = sb("idx_first", [128, 2, CH], I32)
        emb = sb("emb", [128, CH, D])
        emb_first = sb("emb_first", [128, 2, CH, D])
        x0t = sb("x0t", [128, COLS])
        pairs = sb("pairs", [128, L0T, COLS])
        x1f = sb("x1f", [128, COLS])
        x1h = sb("x1h", [128, COLS], F32R)
        x1l = sb("x1l", [128, COLS], F32R)
        x0c = sb("x0c", [128, TILES, FX])
        prods = sb("prods", [128, P_RING, GF * M])
        parts = sb("parts", [128, 2, 2 + DIRECT, GF * M])
        cur1 = sb("cur1", [128, 2, M])
        x0d = sb("x0d", [128, 2, TB, FX])
        gram = sb("gram", [128, FX, B])
        s0 = sb("s0", [128, B])
        s2 = sb("s2", [128, B])
        y_sb = sb("y_sb", [1, B])
        graw = gram[:, :, :].rearrange("p f b -> p (f b)")
        w1raw = graw[:, 0:F * M]
        w0braw = graw[:, F * M:F * M + L0T * M].rearrange("p (t m) -> p t m", m=M)
        w2early = pairs[:, :, :].rearrange("p t n -> p (t n)")
        h1 = prods[:, 0:H1T, :]
        h2 = parts[:, 0, 0:H2T, :]

        def w2_slot(w, i):
            at = M * W2_CHUNK * (i % W2_RING)
            return w[:, at:at + M * (W2_CHUNKS[i][1] - W2_CHUNKS[i][0])]

        def gram_slot(w, f):
            at = M * W2_CHUNK * W2_RING + B * (f % L2_RING)
            return w[:, at:at + B]

        def w2_part(a, b):
            if b <= W2_EARLY:
                return w2early[:, M * a:M * b]
            return w2late[:, M * (a - W2_EARLY):M * (b - W2_EARLY)]

        psd = [ctx.enter_context(nc.psum_tensor(f"psd{i}", [128, 512], F32)) for i in range(D_RING)]
        psa = [ctx.enter_context(nc.psum_tensor(f"psa{i}", [128, 512], F32)) for i in range(A_RING)]
        ps0 = ctx.enter_context(nc.psum_tensor("ps0", [128, 512], F32))
        pst = ctx.enter_context(nc.psum_tensor("pst", [128, 512], F32))
        psg = ctx.enter_context(nc.psum_tensor("psg", [128, 512], F32))

        ids_in, w0_in, w1_in, const_in, mlp_in, w2a_in, w2b_in = (
            sem(n) for n in ("ids_in", "w0_in", "w1_in", "const_in", "mlp_in", "w2a_in", "w2b_in"))
        w0_summed = sem("w0_summed")
        w1h_ready = sem("w1h_ready")
        w1l_ready = sem("w1l_ready")
        ones_ready = sem("ones_ready")
        idx_ready = sem("idx_ready")
        gathered_first = [sem(f"gathered_first{i}") for i in range(2)]
        gathered = sem("gathered")
        scr_written = sem("scr_written")
        loaded = sem("loaded")
        loaded_first = [sem(f"loaded_first{i}") for i in range(len(FIRST_PIECES) - 1)]
        z0_ready = sem("z0_ready")
        l0_done = sem("l0_done")
        tr_done = sem("tr_done")
        x1f_ready = sem("x1f_ready")
        x1h_ready = sem("x1h_ready")
        x1l_ready = sem("x1l_ready")
        x0c_ready = sem("x0c_ready")
        y_d = sem("y_d")
        y_a = sem("y_a")
        acc_steps = sem("acc_steps")
        act_prods = sem("act_prods")
        pool_adds = sem("pool_adds")
        c1_ready = sem("c1_ready")
        x0d_ready = sem("x0d_ready")
        g2_done = sem("g2_done")
        g2_copied = sem("g2_copied")
        w2h_ready = sem("w2h_ready")
        w2l_pool = sem("w2l_pool")
        w2l_dve = sem("w2l_dve")
        gh_ready = sem("gh_ready")
        gl_pool = sem("gl_pool")
        gl_dve = sem("gl_dve")
        l2_steps = sem("l2_steps")
        s2_ready = sem("s2_ready")
        h1_done = sem("h1_done")
        h1_ready = sem("h1_ready")
        h2_done = sem("h2_done")
        h2_ready = sem("h2_ready")
        y_done = sem("y_done")
        y_ready = sem("y_ready")
        stored = sem("stored")

        block = ctx.enter_context(nc.Block())

        @block.sync
        def _(sp):
            def rows_at(row, parts, n):
                return bass.AP(scr_rows.tensor, row * COLS, [[D, parts], [FPC * COLS, n], [1, D]])

            def rows_to_dram(b):
                src = emb
                if starts(b):
                    src = emb_first[:, 0, :, :]
                    sp.wait_ge(gathered_first[0], 16 * CH)
                elif isinstance(b, int) and b == 1:
                    src = emb_first[:, 1, :, :]
                    sp.wait_ge(gathered_first[1], 16 * CH)
                    sp.wait_ge(loaded, 16 * LOAD_DMAS)
                    for done in loaded_first:
                        sp.wait_ge(done, 16 * SPT)
                else:
                    sp.wait_ge(gathered, 16 * CH * (b - 1))
                    sp.wait_ge(loaded, 16 * LOAD_DMAS * b)
                sp.dma_start(rows_at(0, 128, CH - 1), src[:, 0:CH - 1, :]).then_inc(scr_written, 16)
                sp.dma_start(rows_at(FPC * (CH - 1), LAST, 1), src[0:LAST, CH - 1:CH, :]).then_inc(scr_written, 16)
                sp.dma_start(rows_at(F, 128, SHIFTS // FPC), src[:, 0:SHIFTS // FPC, :]).then_inc(scr_written, 16)

            def load_rows(b):
                sp.wait_ge(scr_written, 16 * SCR_DMAS * (b + 1))
                sp.wait_ge(l0_done, b)
                sp.wait_ge(tr_done, b)
                src = bass.AP(scr_rows.tensor, 0, [[0, SPT], [COLS, F], [1, COLS]])
                sp.dma_start(x0t[0:ROWS, :], src).then_inc(loaded, 16)
                for k in range(SPT):
                    n = len(range(k, SHIFTS, SPT))
                    src = bass.AP(scr_rows.tensor, k * COLS, [[COLS, F], [SPT * COLS, n], [1, COLS]])
                    sp.dma_start(pairs[F * k:F * k + F, 0:n, :], src).then_inc(loaded, 16)

            def load_first_rows():
                sp.wait_ge(scr_written, 16 * SCR_DMAS)
                src = bass.AP(scr_rows.tensor, 0, [[0, SPT], [COLS, F], [1, COLS]])
                sp.dma_start(x0t[0:ROWS, :], src).then_inc(loaded, 16)
                for (first, end), done in zip(FIRST_PIECES, [loaded, *loaded_first]):
                    for k in range(SPT):
                        n = min(end, len(range(k, SHIFTS, SPT))) - first
                        src = bass.AP(scr_rows.tensor, (k + SPT * first) * COLS, [[COLS, F], [SPT * COLS, n], [1, COLS]])
                        sp.dma_start(pairs[F * k:F * k + F, first:first + n, :], src).then_inc(done, 16)

            sp.dma_start(ids_sb[:, :], ids).then_inc(ids_in, 16)
            sp.dma_start(base_sb[:, :], base).then_inc(ids_in, 16)
            sp.dma_start(w0s[0:ROWS, :, :], w0a).then_inc(w0_in, 16)
            sp.dma_start(w0braw[F:ROWS, 0, :], w0b[F:ROWS, 0, :]).then_inc(w0_in, 16)
            sp.dma_start(w0braw[0:ROWS, 1:L0T, :], w0b[:, 1:L0T, :]).then_inc(w0_in, 16)
            sp.dma_start(w1raw.rearrange("g (f m) -> g f m", m=M), w1.rearrange("(f g) m -> g f m", g=128)).then_inc(w1_in, 16)
            rows_to_dram(0)
            load_first_rows()
            rows_to_dram(1)
            load_rows(1)
            rows_to_dram(2)
            load_rows(2)
            with sp.Fori(1, NBLK - 2) as b:
                rows_to_dram(b + 2)
                load_rows(b + 2)
            w2v = w2.rearrange("(f g) m -> g f m", g=128)
            sp.dma_start(w2late[:, :].rearrange("g (f m) -> g f m", m=M), w2v[:, W2_EARLY:F, :]).then_inc(w2b_in, 16)
            sp.dma_start(wt1_sb[:, 0:3, :], wt1[0:384, :].rearrange("(k p) n -> p k n", p=128)).then_inc(mlp_in, 16)
            sp.dma_start(wt1_sb[0:16, 3, :], wt1[384:400, :]).then_inc(mlp_in, 16)
            sp.dma_start(wt2_sb[:, :, :], wt2.rearrange("(k p) n -> p k n", p=128)).then_inc(mlp_in, 16)
            sp.wait_ge(l0_done, NBLK)
            sp.dma_start(w2early.rearrange("g (f m) -> g f m", m=M), w2v[:, 0:W2_EARLY, :]).then_inc(w2a_in, 16)
            sp.wait_ge(y_ready, 1)
            sp.dma_start(out.rearrange("b o -> o b"), y_sb[:, :]).then_inc(stored, 16)
            sp.wait_ge(stored, 16)

        @block.gpsimd
        def _(pool):
            def row_numbers(b, at):
                pool.wait_ge(scr_written, 16 * SCR_DMAS * b)
                pool.tensor_tensor(idx[:, :], ids_sb[:, at], base_sb[:, :], ALU.add).then_inc(idx_ready, 1)

            def gather(c):
                n = BB * min(FPC, F - FPC * c)
                pool.indirect_dma_start(emb[0:n, c, :], None, tables,
                                        bass.IndirectOffsetOnAxis(idx[0:n, c:c + 1], 0)).then_inc(gathered, 16)

            def block_of(b, gather_ahead, at=None):
                c = 0
                for t in range(TILES):
                    T = b * TILES + t
                    n_adds = ADD_OFF[t + 1] - ADD_OFF[t]
                    for k in range(max(n_adds, GATHERS_AT[t])):
                        if gather_ahead and t == 0 and k == n_adds - 1:
                            row_numbers(b + 3, at)
                        if k == 1:
                            pool.wait_ge(x0c_ready, T + 1)
                            if t >= 2 or not starts(b):
                                pool.wait_ge(g2_done, T - 1)
                            pool.tensor_tensor(x0d[:, t % 2, :, :],
                                               x0c[:, t, :].unsqueeze(1).to_broadcast([128, TB, FX]),
                                               mask_sb[:, :].unsqueeze(2).to_broadcast([128, TB, FX]),
                                               ALU.mult).then_inc(x0d_ready, 1)
                        if k < n_adds:
                            p = P_OFF[t] + k + 1
                            if k == 0:
                                if t >= 2 or not starts(b):
                                    pool.wait_ge(c1_ready, T - 1)
                            else:
                                pool.wait_ge(pool_adds, b * NADD + ADD_OFF[t] + k)
                            pool.wait_ge(act_prods, b * NA + A_OFF[t] + k + 2)
                            first = prods[:, (p - 1) % P_RING, :] if k == 0 else parts[:, t % 2, 1, :]
                            if gather_ahead and t == 1 and k == 0:
                                pool.wait_ge(idx_ready, b + 4)
                            pool.tensor_tensor(parts[:, t % 2, 1, :], first, prods[:, p % P_RING, :],
                                               ALU.add).then_inc(pool_adds, 1)
                        if gather_ahead and k < GATHERS_AT[t]:
                            gather(c)
                            c += 1

            pool.wait_ge(ids_in, 32)
            for b in range(2):
                pool.tensor_tensor(idx_first[:, b, :], ids_sb[:, b * CH:b * CH + CH], base_sb[:, :], ALU.add).then_inc(idx_ready, 1)
            pool.tensor_tensor(idx[:, :], ids_sb[:, 2 * CH:3 * CH], base_sb[:, :], ALU.add).then_inc(idx_ready, 1)
            pool.memset(x0c[:, :, F:FX], 1.0).then_inc(ones_ready, 1)
            pool.wait_ge(idx_ready, 3)
            for b in range(2):
                for c in range(CH):
                    n = BB * min(FPC, F - FPC * c)
                    pool.indirect_dma_start(emb_first[0:n, b, c, :], None, tables,
                                            bass.IndirectOffsetOnAxis(idx_first[0:n, b, c:c + 1], 0)
                                            ).then_inc(gathered_first[b], 16)
            for c in range(CH):
                gather(c)
            pool.wait_ge(ones_ready, 1)
            pool.wait_ge(const_in, 16 * 5)
            block_of(0, True, slice(3 * CH, 4 * CH))
            with pool.Fori(1, NBLK - 3) as b:
                block_of(b, True, bass.ds((b + 3) * CH, CH))
            block_of(NBLK - 3, False)
            block_of(NBLK - 2, False)
            block_of(NBLK - 1, False)
            pool.wait_ge(w2h_ready, 1)
            pool.tensor_tensor(w2_slot(w1l, 0), w2_part(*W2_CHUNKS[0]), w2_slot(w1h, 0).bitcast(F32),
                               ALU.subtract).then_inc(w2l_pool, 1)
            for f in range(F):
                if on_pool(f):
                    pool.wait_ge(gh_ready, f + 1)
                    if f >= L2_RING:
                        pool.wait_ge(l2_steps, f - L2_RING + 1)
                    pool.tensor_tensor(gram_slot(w1l, f), gram[:, f, :], gram_slot(w1h, f).bitcast(F32),
                                       ALU.subtract).then_inc(gl_pool, 1)

        @block.vector
        def _(dve):
            def z0(b, k):
                if k == 0:
                    dve.wait_ge(loaded, 16 * LOAD_DMAS * (b + 1))
                if starts(b):
                    for (first, end), done in zip(FIRST_PIECES[1:], loaded_first):
                        if k == first:
                            dve.wait_ge(done, 16 * SPT)
                rows = F * len(range(SPT * k, min(SPT * k + SPT, SHIFTS)))
                dve.tensor_tensor(pairs[0:rows, k, :], x0t[0:rows, :], pairs[0:rows, k, :], ALU.mult).then_inc(z0_ready, 1)

            def low_part(b, t):
                dve.wait_ge(x1h_ready, b * TILES + t + 1)
                c = slice(128 * t, 128 * t + 128)
                dve.tensor_tensor(x1l[:, c], x1f[:, c], x1h[:, c].bitcast(F32), ALU.subtract).then_inc(x1l_ready, 1)

            def sum_cur0(b, at):
                dve.wait_ge(x1f_ready, b + 1)
                dve.tensor_reduce(s0[:, at], x1f[:, :].rearrange("p (b d) -> p b d", d=D), AX.X, ALU.add)

            def finish_tile(T, t):
                if not isinstance(T, int) or T >= 2:
                    dve.wait_ge(g2_done, T - 1)
                dve.tensor_reduce(cur1[:, t % 2, :],
                                  parts[:, t % 2, :, :].rearrange("p k (j m) -> p m (k j)", m=M),
                                  AX.X, ALU.add).then_inc(c1_ready, 1)

            def block_of(b, ahead, ahead2, at=None):
                for t in range(TILES):
                    T = b * TILES + t
                    groups = [g for g in range(NG) if PATTERN[t][g] == "d"]
                    for n, g in enumerate(groups):
                        d = D_OFF[t] + n
                        y = psd[d % D_RING]
                        G = b * ND + d
                        dve.wait_ge(y_d, G + 1)
                        if n == 0:
                            dve.wait_ge(x0c_ready, T + 1)
                            dve.tensor_tensor(parts[:, t % 2, 0, :].rearrange("p (j m) -> p j m", m=M),
                                              y[:, :].rearrange("p (j m) -> p j m", m=M),
                                              x0c[:, t, GF * g:GF * g + GF].unsqueeze(2).to_broadcast([128, GF, M]),
                                              ALU.mult).then_inc(acc_steps, 2)
                        else:
                            nf = min(GF, F - GF * g)
                            for j in range(nf):
                                if j == 0:
                                    dve.wait_ge(acc_steps, 2 * G - 1)
                                if j == 2:
                                    dve.wait_ge(acc_steps, 2 * G)
                                acc = parts[:, t % 2, 0, M * j:M * j + M]
                                op = dve.scalar_tensor_tensor(acc, y[:, M * j:M * j + M],
                                                              x0c[:, t, GF * g + j:GF * g + j + 1], acc,
                                                              ALU.mult, ALU.add)
                                if j in (1, nf - 1):
                                    op.then_inc(acc_steps, 1)
                        if n == 0:
                            tp = (t - 1) % TILES
                            bp = b if t else b - 1
                            if t or not starts(b):
                                dve.wait_ge(act_prods, bp * NA + A_OFF[tp + 1])
                                dve.wait_ge(pool_adds, bp * NADD + ADD_OFF[tp + 1])
                                dve.wait_ge(acc_steps, 2 * (bp * ND + D_OFF[tp + 1]))
                                finish_tile(T - 1, tp)
                        if t == 1 and n == 3:
                            low_part(b, TILES - 1)
                        z0_at = Z0_AT_FIRST if starts(b) else Z0_AT
                        if ahead and (t, n) in z0_at:
                            z0(b + 1, z0_at[t, n])
                        if t == 2 and ahead and n == 2:
                            sum_cur0(b + 1, at)
                        if t == 2 and ahead and n == 3:
                            low_part(b + 1, 0)
                            low_part(b + 1, 1)
                        if t == 3 and ahead and n == 1:
                            low_part(b + 1, 2)
                        if ahead2 and t == 3 and 0 < n <= EARLY_Z0:
                            z0(b + 2, n - 1)

            dve.memset(w0braw[0:F, 0, :], 0.0).then_inc(w0_summed, 1)
            dve.wait_ge(w0_summed, 1)
            dve.wait_ge(w0_in, 48)
            dve.tensor_tensor(w0s[0:ROWS, :, :], w0s[0:ROWS, :, :], w0braw[0:ROWS, :, :], ALU.add).then_inc(w0_summed, 1)
            third = F * M // 3
            for k in range(3):
                c = slice(k * third, (k + 1) * third)
                dve.wait_ge(w1h_ready, k + 1)
                dve.tensor_tensor(w1l[:, c], w1raw[:, c], w1h[:, c].bitcast(F32), ALU.subtract).then_inc(w1l_ready, 1)
            for k in range(L0T):
                z0(0, k)
            sum_cur0(0, slice(0, BB))
            for t in range(3):
                low_part(0, t)
            block_of(0, True, True, slice(BB, 2 * BB))
            with dve.Fori(1, NBLK - 2) as b:
                block_of(b, True, True, bass.ds((b + 1) * BB, BB))
            block_of(NBLK - 2, True, False, slice((NBLK - 1) * BB, NBLK * BB))
            block_of(NBLK - 1, False, False)
            dve.wait_ge(act_prods, NBLK * NA)
            dve.wait_ge(pool_adds, NBLK * NADD)
            dve.wait_ge(acc_steps, 2 * NBLK * ND)
            finish_tile(NBLK * TILES - 1, TILES - 1)
            for f in range(F):
                for i in range(1, len(W2_CHUNKS)):
                    if f == W2_CHUNKS[i - 1][0]:
                        dve.wait_ge(w2h_ready, i + 1)
                        if i >= W2_RING:
                            dve.wait_ge(l2_steps, W2_CHUNKS[i - W2_RING][1])
                        dve.tensor_tensor(w2_slot(w1l, i), w2_part(*W2_CHUNKS[i]), w2_slot(w1h, i).bitcast(F32),
                                          ALU.subtract).then_inc(w2l_dve, 1)
                if not on_pool(f):
                    dve.wait_ge(gh_ready, f + 1)
                    if f >= L2_RING:
                        dve.wait_ge(l2_steps, f - L2_RING + 1)
                    dve.tensor_tensor(gram_slot(w1l, f), gram[:, f, :], gram_slot(w1h, f).bitcast(F32),
                                      ALU.subtract).then_inc(gl_dve, 1)

        @block.scalar
        def _(act):
            def load_cur0(b):
                act.wait_ge(l0_done, b + 1)
                if not starts(b):
                    act.wait_ge(x1l_ready, b * TILES)
                act.activation(x1f[:, :], ps0[:, :], ACT.Copy).then_inc(x1f_ready, 1)
                act.wait_ge(x1f_ready, b + 1)

            def high_part(b, t):
                c = slice(128 * t, 128 * t + 128)
                if not starts(b):
                    act.wait_ge(y_d, (b - 1) * ND + D_OFF[t + 1])
                act.activation(x1h[:, c], x1f[:, c], ACT.Copy).then_inc(x1h_ready, 1)

            def scalars(b, t):
                act.wait_ge(tr_done, b + 1)
                if not starts(b):
                    act.wait_ge(acc_steps, 2 * ((b - 1) * ND + D_OFF[t + 1]))
                    act.wait_ge(x0d_ready, (b - 1) * TILES + t + 1)
                act.activation(x0c[:, t, 0:F], pst[:, ROWS * t:ROWS * t + F], ACT.Copy).then_inc(x0c_ready, 1)

            def gram_out(T, at):
                act.wait_ge(g2_done, T + 1)
                act.activation(gram[:, :, at], psg[:, 0:TB * FX].rearrange("p (b f) -> p f b", f=FX),
                               ACT.Copy).then_inc(g2_copied, 1)

            def block_of(b, ahead):
                for t in range(TILES):
                    T = b * TILES + t
                    groups = [g for g in range(NG) if PATTERN[t][g] == "a"]
                    for n, g in enumerate(groups):
                        a = A_OFF[t] + n
                        y = psa[a % A_RING]
                        act.wait_ge(y_a, b * NA + a + 1)
                        if n == 0:
                            act.wait_ge(x0c_ready, T + 1)
                        if n < len(groups) - DIRECT:
                            p = P_OFF[t] + n
                            dst = prods[:, p % P_RING, :]
                            if p >= P_RING:
                                act.wait_ge(pool_adds, b * NADD + adds_before_free(p - P_RING))
                            elif not starts(b):
                                act.wait_ge(pool_adds, (b - 1) * NADD + adds_before_free(p - P_RING + NP))
                        else:
                            dst = parts[:, t % 2, 2 + n - (len(groups) - DIRECT), :]
                            if t >= 2 or not starts(b):
                                act.wait_ge(c1_ready, T - 1)
                        for j in range(GF):
                            op = act.activation(dst[:, M * j:M * j + M], y[:, M * j:M * j + M], ACT.Copy,
                                                scale=x0c[:, t, GF * g + j:GF * g + j + 1])
                        op.then_inc(act_prods, 1)
                        if n == 1 and (t >= 2 or not starts(b)):
                            at = (slice((T - 2) * TB, (T - 1) * TB) if isinstance(T, int)
                                  else bass.ds((T - 2) * TB, TB))
                            gram_out(T - 2, at)
                        if t == 0 and n == 0:
                            high_part(b, 3)
                        if t == 0 and n == 2:
                            scalars(b, 3)
                        if t == 2 and ahead:
                            if n == 2:
                                load_cur0(b + 1)
                            if n == 3:
                                high_part(b + 1, 0)
                                scalars(b + 1, 0)
                            if n == 4:
                                high_part(b + 1, 1)
                            if n == 5:
                                scalars(b + 1, 1)
                        if t == 3 and ahead:
                            if n == 2:
                                high_part(b + 1, 2)
                            if n == 3:
                                scalars(b + 1, 2)

            act.dma_start(ident_sb[0:ROWS, :], ident).then_inc(const_in, 16)
            act.dma_start(mask_sb[:, :], mask).then_inc(const_in, 16)
            act.dma_start(bt1_sb[:, :], bt1).then_inc(const_in, 16)
            act.dma_start(bt2_sb[:, :], bt2).then_inc(const_in, 16)
            act.dma_start(wt3_sb[:, :], wt3).then_inc(const_in, 16)
            act.dma_start(dense_sb[:, :], dense).then_inc(mlp_in, 16)
            act.wait_ge(w1_in, 16)
            third = F * M // 3
            for k in range(3):
                c = slice(k * third, (k + 1) * third)
                act.activation(w1h[:, c], w1raw[:, c], ACT.Copy).then_inc(w1h_ready, 1)
            load_cur0(0)
            for t in range(3):
                high_part(0, t)
            act.wait_ge(w1l_ready, 3)
            for t in range(3):
                scalars(0, t)
            block_of(0, True)
            with act.Fori(1, NBLK - 2) as b:
                block_of(b, True)
            block_of(NBLK - 2, True)
            block_of(NBLK - 1, False)
            def w2_high(i):
                if i >= W2_RING:
                    act.wait_ge(l2_steps, W2_CHUNKS[i - W2_RING][1])
                act.activation(w2_slot(w1h, i), w2_part(*W2_CHUNKS[i]), ACT.Copy).then_inc(w2h_ready, 1)

            act.wait_ge(y_a, NBLK * NA)
            act.wait_ge(y_d, NBLK * ND)
            act.wait_ge(w2a_in, 16)
            act.wait_ge(w2b_in, 16)
            w2_high(0)
            for T in range(NBLK * TILES - 2, NBLK * TILES):
                gram_out(T, slice(T * TB, (T + 1) * TB))
            act.wait_ge(g2_copied, NBLK * TILES)
            for f in range(F):
                for i in range(1, len(W2_CHUNKS)):
                    if f == W2_CHUNKS[i - 1][0]:
                        w2_high(i)
                if f >= L2_RING:
                    act.wait_ge(l2_steps, f - L2_RING + 1)
                act.activation(gram_slot(w1h, f), gram[:, f, :], ACT.Copy).then_inc(gh_ready, 1)
            act.wait_ge(l2_steps, F)
            act.activation(s2[:, :], psg[:, :], ACT.Copy).then_inc(s2_ready, 1)
            act.wait_ge(const_in, 16 * 5)
            act.wait_ge(pool_adds, NBLK * NADD)
            for m, y in enumerate([ps0, pst, psa[0], psa[1]][:H1T]):
                act.wait_ge(h1_done, m + 1)
                act.activation(h1[:, m, :], y[:, :], ACT.Relu, bias=bt1_sb[:, m:m + 1]).then_inc(h1_ready, 1)
            for m in range(H2T):
                act.wait_ge(h2_done, m + 1)
                act.activation(h2[:, m, :], psd[m][:, :], ACT.Relu, bias=bt2_sb[:, m:m + 1]).then_inc(h2_ready, 1)
            act.wait_ge(y_done, 1)
            act.activation(y_sb[:, :], psg[0:1, :], ACT.Copy).then_inc(y_ready, 1)

        @block.tensor
        def _(pe):
            def layer0(b, k):
                if k == 0 and not starts(b):
                    pe.wait_ge(x1f_ready, b)
                pe.wait_ge(z0_ready, b * L0T + k + 1)
                rows = F * len(range(SPT * k, min(SPT * k + SPT, SHIFTS)))
                op = pe.matmul(ps0[:, :], w0s[0:rows, k, :], pairs[0:rows, k, :], start=(k == 0), stop=(k == L0T - 1))
                if k == L0T - 1:
                    op.then_inc(l0_done, 1)

            def turn_x0(b):
                pe.wait_ge(loaded, 16 * LOAD_DMAS * (b + 1))
                if not starts(b):
                    pe.wait_ge(x0c_ready, b * TILES)
                for t in range(TILES):
                    op = pe.transpose(pst[:, ROWS * t:ROWS * t + ROWS], x0t[0:ROWS, 128 * t:128 * t + 128], ident_sb[0:ROWS, :])
                op.then_inc(tr_done, 1)

            def grams(T, t):
                pe.wait_ge(c1_ready, T + 1)
                pe.wait_ge(x0d_ready, T + 1)
                if not isinstance(T, int) or T > 0:
                    pe.wait_ge(g2_copied, T)
                pe.matmul(psg[:, 0:TB * FX], cur1[:, t % 2, :], x0d[:, t % 2, :, :].rearrange("p b f -> p (b f)"),
                          start=True, stop=True).then_inc(g2_done, 1)

            def block_of(b, ahead):
                for t in range(TILES):
                    T = b * TILES + t
                    d, a = D_OFF[t], A_OFF[t]
                    hi, lo = x1h[:, 128 * t:128 * t + 128], x1l[:, 128 * t:128 * t + 128]
                    pe.wait_ge(x1h_ready, T + 1)
                    pe.wait_ge(x1l_ready, T + 1)
                    for g in range(NG):
                        n = M * min(GF, F - GF * g)
                        c = slice(GF * M * g, GF * M * g + n)
                        if PATTERN[t][g] == "d":
                            y, full = psd[d % D_RING], y_d
                            if d >= D_RING or not starts(b):
                                pe.wait_ge(acc_steps, 2 * (b * ND + d - D_RING + 1))
                            d += 1
                        else:
                            y, full = psa[a % A_RING], y_a
                            if a >= A_RING or not starts(b):
                                pe.wait_ge(act_prods, b * NA + a - A_RING + 1)
                            a += 1
                        pe.matmul(y[:, 0:n], hi, w1h[:, c], start=True, stop=False)
                        pe.matmul(y[:, 0:n], hi, w1l[:, c], start=False, stop=False)
                        pe.matmul(y[:, 0:n], lo, w1h[:, c], start=False, stop=True).then_inc(full, 1)
                        if ahead:
                            l0_at = L0_AT_FIRST if starts(b) else L0_AT
                            if (t, g) in l0_at:
                                layer0(b + 1, l0_at[t, g])
                            if t == 1 and g == 5:
                                turn_x0(b + 1)
                        if g == NG - 1 and (t or not starts(b)):
                            grams(T - 1, (t - 1) % TILES)

            pe.wait_ge(w0_summed, 2)
            pe.wait_ge(const_in, 16 * 5)
            for k in range(L0T):
                layer0(0, k)
            turn_x0(0)
            pe.wait_ge(w1h_ready, 3)
            pe.wait_ge(w1l_ready, 3)
            block_of(0, True)
            with pe.Fori(1, NBLK - 2) as b:
                block_of(b, True)
            block_of(NBLK - 2, True)
            block_of(NBLK - 1, False)

            pe.wait_ge(mlp_in, 16 * 4)
            pe.wait_ge(x1f_ready, NBLK)
            pe.wait_ge(x0c_ready, NBLK * TILES)
            banks = [ps0, pst, psa[0], psa[1]][:H1T]
            for m, y in enumerate(banks):
                c = slice(128 * m, 128 * m + 128)
                if m == 2:
                    grams(NBLK * TILES - 1, TILES - 1)
                    pe.wait_ge(act_prods, NBLK * NA)
                pe.matmul(y[:, :], wt1_sb[:, 0, c], s0[:, :], start=True, stop=False)
                pe.matmul(y[:, :], wt1_sb[0:16, 3, c], dense_sb[:, :], start=False, stop=False)

            pe.wait_ge(g2_copied, NBLK * TILES)
            for f in range(F):
                i = f // W2_CHUNK
                if f == W2_CHUNKS[i][0]:
                    pe.wait_ge(w2h_ready, i + 1)
                    if i == 0:
                        pe.wait_ge(w2l_pool, 1)
                    else:
                        pe.wait_ge(w2l_dve, i)
                m = slice(M * (f % W2_CHUNK), M * (f % W2_CHUNK) + M)
                w_high, w_low = w2_slot(w1h, i)[:, m], w2_slot(w1l, i)[:, m]
                pe.wait_ge(gh_ready, f + 1)
                pe.matmul(psg[:, :], w_high, gram_slot(w1h, f), start=(f == 0), stop=False)
                pe.matmul(psg[:, :], w_low, gram_slot(w1h, f), start=False, stop=False)
                if on_pool(f):
                    pe.wait_ge(gl_pool, turn(f, True))
                else:
                    pe.wait_ge(gl_dve, turn(f, False))
                op = pe.matmul(psg[:, :], w_high, gram_slot(w1l, f), start=False, stop=(f == F - 1))
                op.then_inc(l2_steps, 1)

            for m, y in enumerate(banks):
                c = slice(128 * m, 128 * m + 128)
                pe.matmul(y[:, :], wt1_sb[:, 1, c], gram[:, F, :], start=False, stop=False)
            pe.wait_ge(s2_ready, 1)
            for m, y in enumerate(banks):
                c = slice(128 * m, 128 * m + 128)
                pe.matmul(y[:, :], wt1_sb[:, 2, c], s2[:, :], start=False, stop=True).then_inc(h1_done, 1)
            for k in range(H1T):
                pe.wait_ge(h1_ready, k + 1)
                for m in range(H2T):
                    op = pe.matmul(psd[m][:, :], wt2_sb[:, k, 128 * m:128 * m + 128], h1[:, k, :],
                                   start=(k == 0), stop=(k == H1T - 1))
                    if k == H1T - 1:
                        op.then_inc(h2_done, 1)
            for k in range(H2T):
                pe.wait_ge(h2_ready, k + 1)
                op = pe.matmul(psg[0:1, :], wt3_sb[:, k:k + 1], h2[:, k, :], start=(k == 0), stop=(k == H2T - 1))
            op.then_inc(y_done, 1)


def kernel(**inputs):
    import numpy as np
    import concourse.bacc as bacc
    from concourse.bass_utils import run_bass_kernel_spmd

    nc = bacc.Bacc("TRN2", target_bir_lowering=False, num_devices=1)
    arr = {k: np.asarray(v) for k, v in inputs.items()}
    tabs = [arr[f"tbl_{f}"] for f in range(F)]
    start = np.concatenate([[0], np.cumsum([t.shape[0] for t in tabs])])[:F]

    ids = np.concatenate([arr["ids"], arr["ids"][:, 0:CH * FPC - F]], axis=1)
    ids = ids.reshape(NBLK, BB, CH, FPC).transpose(3, 1, 0, 2).reshape(128, NBLK * CH)
    first_row = np.zeros(CH * FPC, np.int32)
    first_row[:F] = start
    base = np.repeat(first_row.reshape(CH, FPC).T, BB, axis=0)

    f_of = np.arange(SPT * L0T * F).reshape(SPT * L0T, F) % F
    g_of = (f_of + np.arange(SPT * L0T)[:, None]) % F
    w0 = arr["L0_rec_f0"]

    def by_tile(rows):
        return np.ascontiguousarray(w0[rows.reshape(-1)].reshape(L0T, ROWS, M).transpose(1, 0, 2))

    samples = np.arange(128)[:, None] // D == np.arange(TB)[None, :]
    arrays = {
        "tables": np.concatenate(tabs, axis=0),
        "ids_by_block": np.ascontiguousarray(ids),
        "first_rows": np.ascontiguousarray(base.astype(np.int32)),
        "w0_pairs": by_tile(f_of * F + g_of),
        "w0_mirrored": by_tile(g_of * F + f_of),
        "w1": arr["L0_rec_f1"],
        "w2": arr["L0_rec_f2"],
        "w_top1": arr["W_top1"],
        "b_top1": np.ascontiguousarray(arr["b_top1"].reshape(-1, 128).T),
        "w_top2": arr["W_top2"],
        "b_top2": np.ascontiguousarray(arr["b_top2"].reshape(-1, 128).T),
        "w_top3": np.ascontiguousarray(arr["W_top3"].reshape(-1, 128).T),
        "dense": np.ascontiguousarray(arr["dense_ctx"].T),
        "sample_mask": samples.astype(np.float32),
        "identity": np.eye(ROWS, dtype=np.float32),
    }
    args = [nc.dram_tensor(k, v.shape, mybir.dt.from_np(v.dtype), kind="ExternalInput").ap() for k, v in arrays.items()]
    out = nc.dram_tensor("out_0", (B, 1), F32, kind="ExternalOutput").ap()
    build(nc, *args, out)
    result = run_bass_kernel_spmd(nc, [arrays], core_ids=[0])
    return result.results[0]["out_0"]
```

```python
from contextlib import ExitStack

import concourse.bass as bass
from concourse import mybir

F32 = mybir.dt.float32
F32R = mybir.dt.float32r
I32 = mybir.dt.int32
ALU = mybir.AluOpType
ACT = mybir.ActivationFunctionType
AX = mybir.AxisListType

B, F, D = 512, 39, 16
M = 128
BB = 32
NBLK = B // BB
COLS = BB * D
TILES = 4
TB = BB // TILES
SHIFTS = (F + 1) // 2
SPT = 3
L0T = -(-SHIFTS // SPT)
ROWS = SPT * F
FPC = 4
CH = -(-F // FPC)
GF = 4
NG = -(-F // GF)
FX = F + 1

PATTERN = ["adaadadaad", "adaadadaad", "adaadadaad", "adaadadaad"]
DIRECT = 2
D_RING, A_RING, P_RING = 2, 3, 4
D_OFF = [sum(p.count("d") for p in PATTERN[:t]) for t in range(TILES + 1)]
A_OFF = [sum(p.count("a") for p in PATTERN[:t]) for t in range(TILES + 1)]
ND, NA = D_OFF[TILES], A_OFF[TILES]
assert ND % D_RING == 0 and NA % A_RING == 0
P_OFF = [A_OFF[t] - DIRECT * t for t in range(TILES + 1)]
NP = P_OFF[TILES]
assert NP % P_RING == 0
ADD_OFF = [P_OFF[t] - t for t in range(TILES + 1)]
NADD = ADD_OFF[TILES]
Z0_AT = {(0, 0): [2], (0, 2): [3], (0, 3): [4], (1, 1): [5], (1, 2): [6]}
L0_AT = {(0, 6): 0, (0, 8): 1, (1, 1): 2, (1, 4): 3, (1, 7): 4, (2, 0): 6, (2, 3): 5}
Z0_AT_FIRST = {(0, 2): [0], (0, 3): [1, 2], (1, 1): [3, 4], (1, 2): [5], (1, 3): [6]}
L0_AT_FIRST = {(1, 2): 0, (1, 4): 1, (1, 6): 2, (1, 9): 3, (2, 1): 4, (2, 2): 6, (2, 4): 5}
WARMING = 3
SPLIT = [2, 3, 4, 5]
ON_POOL = SPLIT[0]
L0_END = 5
NS = len(SPLIT)
ZL_POOL_AT = (0, 1)
ZL_POOL_AT_FIRST = (1, 0)
ZH_AT = {(0, 3): 2, (0, 5): 3, (1, 0): 4, (1, 2): 5}
ZL_AT = {(0, 3): 3, (1, 0): 4, (1, 3): 5}
ZH_AT_FIRST = {(1, 1): 2, (1, 3): 3, (1, 4): 4, (1, 5): 5}
ZL_AT_FIRST = {(1, 2): 3, (1, 3): 4, (2, 0): 5}
assert all(sorted(at.values()) == SPLIT for at in (ZH_AT, ZH_AT_FIRST))
CUR0_AT, SUM_AT = (2, 3), (2, 3)
HIGH_AT = {(2, 4): 0, (3, 0): 1, (3, 2): 2}
SCALARS_AT = {(2, 5): 0, (3, 1): 1, (3, 3): 2}
LOW_AT = {(2, 3): 0, (3, 1): 1, (3, 2): 2}
EARLY_Z0_AT = {(3, 2): 0, (3, 3): 1}
FIRST_PIECES = [(0, 1), (1, 3), (3, 5), (5, L0T)]
GATHERS_AT = [0, 4, 3, 3]
GATHERS_AT_FIRST = [0, 0, 5, 5]
LAST = BB * (F - FPC * (CH - 1))
assert BB * FPC == 128 and SHIFTS % FPC == 0
SCR_DMAS, LOAD_DMAS = 3, 4
W2_EARLY = 28
W2_CHUNK, W2_RING = 7, 3
W2_CHUNKS = [(f, min(f + W2_CHUNK, F)) for f in range(0, F, W2_CHUNK)]
W2_AHEAD = 3
L2_RING = 4
assert W2_EARLY % W2_CHUNK == 0 and W2_RING * W2_CHUNK * M + L2_RING * B <= F * M


def on_pool(f):
    return f % 4 == 3


def turn(f, pool):
    return sum(on_pool(i) == pool for i in range(f + 1))


def adds_before_free(p):
    t = max(t for t in range(TILES) if P_OFF[t] <= p)
    return ADD_OFF[t] + max(p - P_OFF[t], 1)


def starts(b):
    return isinstance(b, int) and b == 0


def build(nc, tables, ids, w0a, w0b, w1, w2, wt1, bt1, wt2, bt2, wt3, dense, mask, ident, out):
    scratch = nc.dram_tensor("x0_rows", (F + SHIFTS, BB, D), F32, kind="Internal").ap()
    scr_rows = scratch.rearrange("f b d -> f (b d)")
    H1T, H2T = wt1.shape[1] // 128, wt2.shape[1] // 128

    with ExitStack() as ctx:
        def sb(name, shape, dt=F32):
            return ctx.enter_context(nc.sbuf_tensor(name, shape, dt))

        def sem(name):
            return ctx.enter_context(nc.semaphore(name))

        w1h = sb("w1h", [128, F * M], F32R)
        w1l = sb("w1l", [128, F * M], F32R)
        w0s = sb("w0s", [128, L0T, M])
        wt1_sb = sb("wt1_sb", [128, 4, H1T * 128])
        w0h = sb("w0h", [128, NS * M], F32R)
        w0l = sb("w0l", [128, NS * M], F32R)
        wt3_sb = sb("wt3_sb", [128, H2T])
        bt1_sb = sb("bt1_sb", [128, H1T])
        bt2_sb = sb("bt2_sb", [128, H2T])
        mask_sb = sb("mask_sb", [128, TB])
        ident_sb = sb("ident_sb", [128, ROWS])
        ids_sb = sb("ids_sb", [128, (NBLK + 1) * CH], I32)
        base_sb = ids_sb[:, NBLK * CH:(NBLK + 1) * CH]
        idx = sb("idx", [128, CH], I32)
        idx_first = sb("idx_first", [128, 2, CH], I32)
        emb = sb("emb", [128, CH, D])
        emb_first = sb("emb_first", [128, 2, CH, D])
        x0t = sb("x0t", [128, COLS])
        pairs = sb("pairs", [128, L0T, COLS])
        z0h = sb("z0h", [128, NS * COLS], F32R)
        z0l = sb("z0l", [128, NS * COLS], F32R)
        x1f = sb("x1f", [128, COLS])
        x1h = sb("x1h", [128, COLS], F32R)
        x1l = sb("x1l", [128, COLS], F32R)
        x0c = sb("x0c", [128, TILES, FX])
        prods = sb("prods", [128, P_RING, GF * M])
        parts = sb("parts", [128, 2, 2 + DIRECT, GF * M])
        cur1 = sb("cur1", [128, 2, M])
        x0d = sb("x0d", [128, 2, TB, FX])
        gram = sb("gram", [128, FX, B])
        s0 = sb("s0", [128, B])
        graw = gram[:, :, :].rearrange("p f b -> p (f b)")
        w1raw = graw[:, 0:F * M]
        w0braw = graw[:, F * M:F * M + L0T * M].rearrange("p (t m) -> p t m", m=M)
        w2early = pairs[:, :, :].rearrange("p t n -> p (t n)")
        w2late = prods[:, :, :].rearrange("p k n -> p (k n)")[:, 0:(F - W2_EARLY) * M]
        h1 = prods[:, 0:H1T, :]
        h2 = parts[:, 0, 0:H2T, :]
        wt2_sb = parts[:, 1, 0:H1T * H2T * 128 // B, :].rearrange("p a n -> p (a n)").rearrange("p (k n) -> p k n", k=H1T)
        dense_sb = x0t[0:16, :]
        s2 = x1f
        y_sb = s0[0:1, :]

        def w2_slot(w, i):
            at = M * W2_CHUNK * (i % W2_RING)
            return w[:, at:at + M * (W2_CHUNKS[i][1] - W2_CHUNKS[i][0])]

        def gram_slot(w, f):
            at = M * W2_CHUNK * W2_RING + B * (f % L2_RING)
            return w[:, at:at + B]

        def w2_part(a, b):
            if b <= W2_EARLY:
                return w2early[:, M * a:M * b]
            return w2late[:, M * (a - W2_EARLY):M * (b - W2_EARLY)]

        psd = [ctx.enter_context(nc.psum_tensor(f"psd{i}", [128, 512], F32)) for i in range(D_RING)]
        psa = [ctx.enter_context(nc.psum_tensor(f"psa{i}", [128, 512], F32)) for i in range(A_RING)]
        ps0 = ctx.enter_context(nc.psum_tensor("ps0", [128, 512], F32))
        pst = ctx.enter_context(nc.psum_tensor("pst", [128, 512], F32))
        psg = ctx.enter_context(nc.psum_tensor("psg", [128, 512], F32))

        ids_in, w0_in, w1_in, const_in, mlp_in, wt2_in, w2a_in, w2b_in = (
            sem(n) for n in ("ids_in", "w0_in", "w1_in", "const_in", "mlp_in", "wt2_in", "w2a_in", "w2b_in"))
        w0_summed = sem("w0_summed")
        w1h_ready = sem("w1h_ready")
        w1l_ready = sem("w1l_ready")
        ones_ready = sem("ones_ready")
        idx_ready = sem("idx_ready")
        gathered_first = [sem(f"gathered_first{i}") for i in range(2)]
        gathered = sem("gathered")
        scr_written = sem("scr_written")
        loaded = sem("loaded")
        loaded_first = [sem(f"loaded_first{i}") for i in range(len(FIRST_PIECES) - 1)]
        z0_ready = sem("z0_ready")
        w0h_ready = sem("w0h_ready")
        w0l_ready = sem("w0l_ready")
        z0h_ready = sem("z0h_ready")
        z0l_ready = sem("z0l_ready")
        z0l_pool = sem("z0l_pool")
        l0_done = sem("l0_done")
        tr_done = sem("tr_done")
        x1f_ready = sem("x1f_ready")
        x1h_ready = sem("x1h_ready")
        x1l_ready = sem("x1l_ready")
        x0c_ready = sem("x0c_ready")
        y_d = sem("y_d")
        y_a = sem("y_a")
        acc_steps = sem("acc_steps")
        act_prods = sem("act_prods")
        pool_adds = sem("pool_adds")
        c1_ready = sem("c1_ready")
        x0d_ready = sem("x0d_ready")
        g2_done = sem("g2_done")
        g2_copied = sem("g2_copied")
        w2h_ready = sem("w2h_ready")
        w2l_pool = sem("w2l_pool")
        w2l_dve = sem("w2l_dve")
        gh_ready = sem("gh_ready")
        gl_pool = sem("gl_pool")
        gl_dve = sem("gl_dve")
        l2_steps = sem("l2_steps")
        s2_ready = sem("s2_ready")
        h1_done = sem("h1_done")
        h1_ready = sem("h1_ready")
        h2_done = sem("h2_done")
        h2_ready = sem("h2_ready")
        y_done = sem("y_done")
        y_ready = sem("y_ready")
        stored = sem("stored")

        block = ctx.enter_context(nc.Block())

        @block.sync
        def _(sp):
            def rows_at(row, parts, n):
                return bass.AP(scr_rows.tensor, row * COLS, [[D, parts], [FPC * COLS, n], [1, D]])

            def rows_to_dram(b):
                src = emb
                if starts(b):
                    src = emb_first[:, 0, :, :]
                    sp.wait_ge(gathered_first[0], 16 * CH)
                elif isinstance(b, int) and b == 1:
                    src = emb_first[:, 1, :, :]
                    sp.wait_ge(gathered_first[1], 16 * CH)
                    sp.wait_ge(loaded, 16 * LOAD_DMAS)
                    for done in loaded_first:
                        sp.wait_ge(done, 16 * SPT)
                else:
                    sp.wait_ge(gathered, 16 * CH * (b - 1))
                    sp.wait_ge(loaded, 16 * LOAD_DMAS * b)
                sp.dma_start(rows_at(0, 128, CH - 1), src[:, 0:CH - 1, :]).then_inc(scr_written, 16)
                sp.dma_start(rows_at(FPC * (CH - 1), LAST, 1), src[0:LAST, CH - 1:CH, :]).then_inc(scr_written, 16)
                sp.dma_start(rows_at(F, 128, SHIFTS // FPC), src[:, 0:SHIFTS // FPC, :]).then_inc(scr_written, 16)

            def load_rows(b):
                sp.wait_ge(scr_written, 16 * SCR_DMAS * (b + 1))
                sp.wait_ge(l0_done, b)
                sp.wait_ge(tr_done, b)
                src = bass.AP(scr_rows.tensor, 0, [[0, SPT], [COLS, F], [1, COLS]])
                sp.dma_start(x0t[0:ROWS, :], src).then_inc(loaded, 16)
                for k in range(SPT):
                    n = len(range(k, SHIFTS, SPT))
                    src = bass.AP(scr_rows.tensor, k * COLS, [[COLS, F], [SPT * COLS, n], [1, COLS]])
                    sp.dma_start(pairs[F * k:F * k + F, 0:n, :], src).then_inc(loaded, 16)

            def load_first_rows():
                sp.wait_ge(scr_written, 16 * SCR_DMAS)
                src = bass.AP(scr_rows.tensor, 0, [[0, SPT], [COLS, F], [1, COLS]])
                sp.dma_start(x0t[0:ROWS, :], src).then_inc(loaded, 16)
                for (first, end), done in zip(FIRST_PIECES, [loaded, *loaded_first]):
                    for k in range(SPT):
                        n = min(end, len(range(k, SHIFTS, SPT))) - first
                        src = bass.AP(scr_rows.tensor, (k + SPT * first) * COLS, [[COLS, F], [SPT * COLS, n], [1, COLS]])
                        sp.dma_start(pairs[F * k:F * k + F, first:first + n, :], src).then_inc(done, 16)

            sp.dma_start(ids_sb[:, :], ids).then_inc(ids_in, 16)
            sp.dma_start(w0s[0:ROWS, :, :], w0a).then_inc(w0_in, 16)
            sp.dma_start(w0braw[F:ROWS, 0, :], w0b[F:ROWS, 0, :]).then_inc(w0_in, 16)
            sp.dma_start(w0braw[0:ROWS, 1:L0T, :], w0b[:, 1:L0T, :]).then_inc(w0_in, 16)
            sp.dma_start(w1raw.rearrange("g (f m) -> g f m", m=M), w1.rearrange("(f g) m -> g f m", g=128)).then_inc(w1_in, 16)
            rows_to_dram(0)
            load_first_rows()
            rows_to_dram(1)
            load_rows(1)
            rows_to_dram(2)
            load_rows(2)
            with sp.Fori(1, NBLK - 2) as b:
                rows_to_dram(b + 2)
                load_rows(b + 2)
            w2v = w2.rearrange("(f g) m -> g f m", g=128)
            sp.dma_start(wt1_sb[:, 0:3, :], wt1[0:384, :].rearrange("(k p) n -> p k n", p=128)).then_inc(mlp_in, 16)
            sp.dma_start(wt1_sb[0:16, 3, :], wt1[384:400, :]).then_inc(mlp_in, 16)
            sp.wait_ge(l0_done, NBLK)
            sp.dma_start(w2early.rearrange("g (f m) -> g f m", m=M), w2v[:, 0:W2_EARLY, :]).then_inc(w2a_in, 16)
            sp.wait_ge(tr_done, NBLK)
            sp.dma_start(dense_sb, dense).then_inc(mlp_in, 16)
            sp.wait_ge(pool_adds, NBLK * NADD)
            sp.dma_start(w2late.rearrange("g (f m) -> g f m", m=M), w2v[:, W2_EARLY:F, :]).then_inc(w2b_in, 16)
            sp.wait_ge(c1_ready, NBLK * TILES)
            sp.dma_start(wt2_sb, wt2.rearrange("(k p) n -> p k n", p=128)).then_inc(wt2_in, 16)
            sp.wait_ge(y_ready, 1)
            sp.dma_start(out.rearrange("b o -> o b"), y_sb[:, :]).then_inc(stored, 16)
            sp.wait_ge(stored, 16)

        @block.gpsimd
        def _(pool):
            def row_numbers(b, at):
                pool.wait_ge(scr_written, 16 * SCR_DMAS * b)
                pool.tensor_tensor(idx[:, :], ids_sb[:, at], base_sb, ALU.add).then_inc(idx_ready, 1)

            def gather(c):
                n = BB * min(FPC, F - FPC * c)
                pool.indirect_dma_start(emb[0:n, c, :], None, tables,
                                        bass.IndirectOffsetOnAxis(idx[0:n, c:c + 1], 0)).then_inc(gathered, 16)

            def block_of(b, ahead, gather_ahead, at=None):
                c = 0
                gathers = GATHERS_AT_FIRST if starts(b) else GATHERS_AT
                first_tile = min(t for t in range(TILES) if gathers[t])
                for t in range(TILES):
                    T = b * TILES + t
                    n_adds = ADD_OFF[t + 1] - ADD_OFF[t]
                    for k in range(max(n_adds, gathers[t])):
                        if gather_ahead and t == first_tile - 1 and k == n_adds - 1:
                            row_numbers(b + 3, at)
                        if k == 1:
                            pool.wait_ge(x0c_ready, T + 1)
                            if t >= 2 or not starts(b):
                                pool.wait_ge(g2_done, T - 1)
                            pool.tensor_tensor(x0d[:, t % 2, :, :],
                                               x0c[:, t, :].unsqueeze(1).to_broadcast([128, TB, FX]),
                                               mask_sb[:, :].unsqueeze(2).to_broadcast([128, TB, FX]),
                                               ALU.mult).then_inc(x0d_ready, 1)
                        if k < n_adds:
                            p = P_OFF[t] + k + 1
                            if k == 0:
                                if t >= 2 or not starts(b):
                                    pool.wait_ge(c1_ready, T - 1)
                            else:
                                pool.wait_ge(pool_adds, b * NADD + ADD_OFF[t] + k)
                            pool.wait_ge(act_prods, b * NA + A_OFF[t] + k + 2)
                            first = prods[:, (p - 1) % P_RING, :] if k == 0 else parts[:, t % 2, 1, :]
                            if gather_ahead and t == first_tile and k == 0:
                                pool.wait_ge(idx_ready, b + 4)
                            pool.tensor_tensor(parts[:, t % 2, 1, :], first, prods[:, p % P_RING, :],
                                               ALU.add).then_inc(pool_adds, 1)
                        if ahead and (t, k) == (ZL_POOL_AT_FIRST if starts(b) else ZL_POOL_AT):
                            pool.wait_ge(z0h_ready, b * NS + 1)
                            pool.tensor_tensor(z0l[0:ROWS, 0:COLS], pairs[0:ROWS, ON_POOL, :],
                                               z0h[0:ROWS, 0:COLS].bitcast(F32), ALU.subtract).then_inc(z0l_pool, 1)
                        if gather_ahead and k < gathers[t]:
                            gather(c)
                            c += 1

            pool.wait_ge(ids_in, 16)
            for b in range(2):
                pool.tensor_tensor(idx_first[:, b, :], ids_sb[:, b * CH:b * CH + CH], base_sb, ALU.add).then_inc(idx_ready, 1)
                pool.wait_ge(idx_ready, b + 1)
                for c in range(CH):
                    n = BB * min(FPC, F - FPC * c)
                    pool.indirect_dma_start(emb_first[0:n, b, c, :], None, tables,
                                            bass.IndirectOffsetOnAxis(idx_first[0:n, b, c:c + 1], 0)
                                            ).then_inc(gathered_first[b], 16)
            pool.tensor_tensor(idx[:, :], ids_sb[:, 2 * CH:3 * CH], base_sb, ALU.add).then_inc(idx_ready, 1)
            pool.memset(x0c[:, :, F:FX], 1.0).then_inc(ones_ready, 1)
            pool.wait_ge(idx_ready, 3)
            for c in range(CH):
                gather(c)
            pool.wait_ge(ones_ready, 1)
            pool.wait_ge(const_in, 16 * 5)
            block_of(0, True, True, slice(3 * CH, 4 * CH))
            with pool.Fori(1, NBLK - 3) as b:
                block_of(b, True, True, bass.ds((b + 3) * CH, CH))
            block_of(NBLK - 3, True, False)
            block_of(NBLK - 2, True, False)
            block_of(NBLK - 1, False, False)
            pool.wait_ge(w2h_ready, 1)
            pool.tensor_tensor(w2_slot(w1l, 0), w2_part(*W2_CHUNKS[0]), w2_slot(w1h, 0).bitcast(F32),
                               ALU.subtract).then_inc(w2l_pool, 1)
            for f in range(F):
                if on_pool(f):
                    pool.wait_ge(gh_ready, f + 1)
                    if f >= L2_RING:
                        pool.wait_ge(l2_steps, f - L2_RING + 1)
                    pool.tensor_tensor(gram_slot(w1l, f), gram[:, f, :], gram_slot(w1h, f).bitcast(F32),
                                       ALU.subtract).then_inc(gl_pool, 1)

        @block.vector
        def _(dve):
            def z0(b, k):
                if k == 0:
                    dve.wait_ge(loaded, 16 * LOAD_DMAS * (b + 1))
                if starts(b):
                    for (first, end), done in zip(FIRST_PIECES[1:], loaded_first):
                        if k == first:
                            dve.wait_ge(done, 16 * SPT)
                rows = F * len(range(SPT * k, min(SPT * k + SPT, SHIFTS)))
                dve.tensor_tensor(pairs[0:rows, k, :], x0t[0:rows, :], pairs[0:rows, k, :], ALU.mult).then_inc(z0_ready, 1)

            def pair_low_part(b, k):
                i = SPLIT.index(k)
                dve.wait_ge(z0h_ready, (b - 1) * NS + i + 1)
                c = slice(COLS * i, COLS * i + COLS)
                dve.tensor_tensor(z0l[0:ROWS, c], pairs[0:ROWS, k, :], z0h[0:ROWS, c].bitcast(F32),
                                  ALU.subtract).then_inc(z0l_ready, 1)

            def low_part(b, t):
                dve.wait_ge(x1h_ready, b * TILES + t + 1)
                c = slice(128 * t, 128 * t + 128)
                dve.tensor_tensor(x1l[:, c], x1f[:, c], x1h[:, c].bitcast(F32), ALU.subtract).then_inc(x1l_ready, 1)

            def sum_cur0(b, at):
                dve.wait_ge(x1f_ready, b + 1)
                dve.tensor_reduce(s0[:, at], x1f[:, :].rearrange("p (b d) -> p b d", d=D), AX.X, ALU.add)

            def finish_tile(T, t):
                if not isinstance(T, int) or T >= 2:
                    dve.wait_ge(g2_done, T - 1)
                dve.tensor_reduce(cur1[:, t % 2, :],
                                  parts[:, t % 2, :, :].rearrange("p k (j m) -> p m (k j)", m=M),
                                  AX.X, ALU.add).then_inc(c1_ready, 1)

            def block_of(b, ahead, ahead2, at=None):
                for t in range(TILES):
                    T = b * TILES + t
                    groups = [g for g in range(NG) if PATTERN[t][g] == "d"]
                    for n, g in enumerate(groups):
                        d = D_OFF[t] + n
                        y = psd[d % D_RING]
                        G = b * ND + d
                        dve.wait_ge(y_d, G + 1)
                        if n == 0:
                            dve.wait_ge(x0c_ready, T + 1)
                            dve.tensor_tensor(parts[:, t % 2, 0, :].rearrange("p (j m) -> p j m", m=M),
                                              y[:, :].rearrange("p (j m) -> p j m", m=M),
                                              x0c[:, t, GF * g:GF * g + GF].unsqueeze(2).to_broadcast([128, GF, M]),
                                              ALU.mult).then_inc(acc_steps, 2)
                        else:
                            nf = min(GF, F - GF * g)
                            for j in range(nf):
                                if j == 0:
                                    dve.wait_ge(acc_steps, 2 * G - 1)
                                if j == 2:
                                    dve.wait_ge(acc_steps, 2 * G)
                                acc = parts[:, t % 2, 0, M * j:M * j + M]
                                op = dve.scalar_tensor_tensor(acc, y[:, M * j:M * j + M],
                                                              x0c[:, t, GF * g + j:GF * g + j + 1], acc,
                                                              ALU.mult, ALU.add)
                                if j in (1, nf - 1):
                                    op.then_inc(acc_steps, 1)
                        if n == 0:
                            tp = (t - 1) % TILES
                            bp = b if t else b - 1
                            if t or not starts(b):
                                dve.wait_ge(act_prods, bp * NA + A_OFF[tp + 1])
                                dve.wait_ge(pool_adds, bp * NADD + ADD_OFF[tp + 1])
                                dve.wait_ge(acc_steps, 2 * (bp * ND + D_OFF[tp + 1]))
                                finish_tile(T - 1, tp)
                        if t == 1 and n == 3:
                            low_part(b, TILES - 1)
                        z0_at = Z0_AT_FIRST if starts(b) else Z0_AT
                        if ahead:
                            for k in z0_at.get((t, n), []):
                                z0(b + 1, k)
                            zl_at = ZL_AT_FIRST if starts(b) else ZL_AT
                            if (t, n) in zl_at:
                                pair_low_part(b + 1, zl_at[t, n])
                        if ahead and (t, n) == SUM_AT:
                            sum_cur0(b + 1, at)
                        if ahead and (t, n) in LOW_AT:
                            low_part(b + 1, LOW_AT[t, n])
                        if ahead2 and (t, n) in EARLY_Z0_AT:
                            z0(b + 2, EARLY_Z0_AT[t, n])

            dve.memset(w0braw[0:F, 0, :], 0.0).then_inc(w0_summed, 1)
            dve.wait_ge(w0_summed, 1)
            dve.wait_ge(w0_in, 48)
            dve.tensor_tensor(w0s[0:ROWS, :, :], w0s[0:ROWS, :, :], w0braw[0:ROWS, :, :], ALU.add).then_inc(w0_summed, 1)
            split_w0 = w0s[0:ROWS, SPLIT[0]:SPLIT[-1] + 1, :].rearrange("p t m -> p (t m)")
            dve.wait_ge(w0h_ready, 1)
            dve.tensor_tensor(w0l[0:ROWS, :], split_w0, w0h[0:ROWS, :].bitcast(F32), ALU.subtract).then_inc(w0l_ready, 1)
            third = F * M // 3
            for k in range(3):
                c = slice(k * third, (k + 1) * third)
                dve.wait_ge(w1h_ready, k + 1)
                dve.tensor_tensor(w1l[:, c], w1raw[:, c], w1h[:, c].bitcast(F32), ALU.subtract).then_inc(w1l_ready, 1)
            for k in range(L0T):
                z0(0, k)
            for t in range(3):
                low_part(0, t)
            sum_cur0(0, slice(0, BB))
            block_of(0, True, True, slice(BB, 2 * BB))
            with dve.Fori(1, NBLK - 2) as b:
                block_of(b, True, True, bass.ds((b + 1) * BB, BB))
            block_of(NBLK - 2, True, False, slice((NBLK - 1) * BB, NBLK * BB))
            block_of(NBLK - 1, False, False)
            dve.wait_ge(act_prods, NBLK * NA)
            dve.wait_ge(pool_adds, NBLK * NADD)
            dve.wait_ge(acc_steps, 2 * NBLK * ND)
            finish_tile(NBLK * TILES - 1, TILES - 1)
            for f in range(F):
                for i in range(1, len(W2_CHUNKS)):
                    if f == (W2_CHUNKS[i - 1][0] - W2_AHEAD if i > 1 else 0):
                        dve.wait_ge(w2h_ready, i + 1)
                        if i >= W2_RING:
                            dve.wait_ge(l2_steps, W2_CHUNKS[i - W2_RING][1])
                        dve.tensor_tensor(w2_slot(w1l, i), w2_part(*W2_CHUNKS[i]), w2_slot(w1h, i).bitcast(F32),
                                          ALU.subtract).then_inc(w2l_dve, 1)
                if not on_pool(f):
                    dve.wait_ge(gh_ready, f + 1)
                    if f >= L2_RING:
                        dve.wait_ge(l2_steps, f - L2_RING + 1)
                    dve.tensor_tensor(gram_slot(w1l, f), gram[:, f, :], gram_slot(w1h, f).bitcast(F32),
                                      ALU.subtract).then_inc(gl_dve, 1)

        @block.scalar
        def _(act):
            def load_cur0(b):
                act.wait_ge(l0_done, b + 1)
                if not starts(b):
                    act.wait_ge(x1l_ready, b * TILES)
                act.activation(x1f[:, :], ps0[:, :], ACT.Copy).then_inc(x1f_ready, 1)
                act.wait_ge(x1f_ready, b + 1)

            def pair_high_part(b, k):
                i = SPLIT.index(k)
                act.wait_ge(z0_ready, b * L0T + k + 1)
                act.wait_ge(l0_done, b)
                c = slice(COLS * i, COLS * i + COLS)
                act.activation(z0h[0:ROWS, c], pairs[0:ROWS, k, :], ACT.Copy).then_inc(z0h_ready, 1)

            def high_part(b, t):
                c = slice(128 * t, 128 * t + 128)
                if not starts(b):
                    act.wait_ge(y_d, (b - 1) * ND + D_OFF[t + 1])
                act.activation(x1h[:, c], x1f[:, c], ACT.Copy).then_inc(x1h_ready, 1)

            def scalars(b, t):
                act.wait_ge(tr_done, b + 1)
                if not starts(b):
                    act.wait_ge(acc_steps, 2 * ((b - 1) * ND + D_OFF[t + 1]))
                    act.wait_ge(x0d_ready, (b - 1) * TILES + t + 1)
                act.activation(x0c[:, t, 0:F], pst[:, ROWS * t:ROWS * t + F], ACT.Copy).then_inc(x0c_ready, 1)

            def gram_out(T, at):
                act.wait_ge(g2_done, T + 1)
                act.activation(gram[:, :, at], psg[:, 0:TB * FX].rearrange("p (b f) -> p f b", f=FX),
                               ACT.Copy).then_inc(g2_copied, 1)

            def block_of(b, ahead):
                for t in range(TILES):
                    T = b * TILES + t
                    groups = [g for g in range(NG) if PATTERN[t][g] == "a"]
                    for n, g in enumerate(groups):
                        a = A_OFF[t] + n
                        y = psa[a % A_RING]
                        act.wait_ge(y_a, b * NA + a + 1)
                        if n == 0:
                            act.wait_ge(x0c_ready, T + 1)
                        if n < len(groups) - DIRECT:
                            p = P_OFF[t] + n
                            dst = prods[:, p % P_RING, :]
                            if p >= P_RING:
                                act.wait_ge(pool_adds, b * NADD + adds_before_free(p - P_RING))
                            elif not starts(b):
                                act.wait_ge(pool_adds, (b - 1) * NADD + adds_before_free(p - P_RING + NP))
                        else:
                            dst = parts[:, t % 2, 2 + n - (len(groups) - DIRECT), :]
                            if t >= 2 or not starts(b):
                                act.wait_ge(c1_ready, T - 1)
                        for j in range(GF):
                            op = act.activation(dst[:, M * j:M * j + M], y[:, M * j:M * j + M], ACT.Copy,
                                                scale=x0c[:, t, GF * g + j:GF * g + j + 1])
                        op.then_inc(act_prods, 1)
                        if n == 1 and (t >= 2 or not starts(b)):
                            at = (slice((T - 2) * TB, (T - 1) * TB) if isinstance(T, int)
                                  else bass.ds((T - 2) * TB, TB))
                            gram_out(T - 2, at)
                        zh_at = ZH_AT_FIRST if starts(b) else ZH_AT
                        if ahead and (t, n) in zh_at:
                            pair_high_part(b + 1, zh_at[t, n])
                        if t == 0 and n == 0:
                            high_part(b, 3)
                        if t == 0 and n == 2:
                            scalars(b, 3)
                        if ahead:
                            if (t, n) == CUR0_AT:
                                load_cur0(b + 1)
                            if (t, n) in HIGH_AT:
                                high_part(b + 1, HIGH_AT[t, n])
                            if (t, n) in SCALARS_AT:
                                scalars(b + 1, SCALARS_AT[t, n])

            act.dma_start(ident_sb[0:ROWS, :], ident).then_inc(const_in, 16)
            act.dma_start(mask_sb[:, :], mask).then_inc(const_in, 16)
            act.dma_start(bt1_sb[:, :], bt1).then_inc(const_in, 16)
            act.dma_start(bt2_sb[:, :], bt2).then_inc(const_in, 16)
            act.dma_start(wt3_sb[:, :], wt3).then_inc(const_in, 16)
            split_w0 = w0s[0:ROWS, SPLIT[0]:SPLIT[-1] + 1, :].rearrange("p t m -> p (t m)")
            act.wait_ge(w0_summed, 2)
            act.activation(w0h[0:ROWS, :], split_w0, ACT.Copy).then_inc(w0h_ready, 1)
            act.wait_ge(w1_in, 16)
            third = F * M // 3
            for k in range(3):
                c = slice(k * third, (k + 1) * third)
                act.activation(w1h[:, c], w1raw[:, c], ACT.Copy).then_inc(w1h_ready, 1)
            load_cur0(0)
            for t in range(3):
                high_part(0, t)
            act.wait_ge(w1l_ready, 3)
            for t in range(3):
                scalars(0, t)
            block_of(0, True)
            with act.Fori(1, NBLK - 2) as b:
                block_of(b, True)
            block_of(NBLK - 2, True)
            block_of(NBLK - 1, False)
            def w2_high(i):
                if i >= W2_RING:
                    act.wait_ge(l2_steps, W2_CHUNKS[i - W2_RING][1])
                if W2_CHUNKS[i][0] == W2_EARLY:
                    act.wait_ge(w2b_in, 16)
                act.activation(w2_slot(w1h, i), w2_part(*W2_CHUNKS[i]), ACT.Copy).then_inc(w2h_ready, 1)

            act.wait_ge(y_a, NBLK * NA)
            act.wait_ge(y_d, NBLK * ND)
            act.wait_ge(w2a_in, 16)
            w2_high(0)
            for T in range(NBLK * TILES - 2, NBLK * TILES):
                gram_out(T, slice(T * TB, (T + 1) * TB))
                if T == NBLK * TILES - 2:
                    w2_high(1)
            act.wait_ge(g2_copied, NBLK * TILES)
            for f in range(F):
                for i in range(2, len(W2_CHUNKS)):
                    if f == W2_CHUNKS[i - 1][0] - W2_AHEAD:
                        w2_high(i)
                if f >= L2_RING:
                    act.wait_ge(l2_steps, f - L2_RING + 1)
                act.activation(gram_slot(w1h, f), gram[:, f, :], ACT.Copy).then_inc(gh_ready, 1)
            act.wait_ge(l2_steps, F)
            act.activation(s2[:, :], psg[:, :], ACT.Copy).then_inc(s2_ready, 1)
            act.wait_ge(const_in, 16 * 5)
            act.wait_ge(pool_adds, NBLK * NADD)
            for m, y in enumerate([ps0, pst, psa[0], psa[1]][:H1T]):
                act.wait_ge(h1_done, m + 1)
                act.activation(h1[:, m, :], y[:, :], ACT.Relu, bias=bt1_sb[:, m:m + 1]).then_inc(h1_ready, 1)
            for m in range(H2T):
                act.wait_ge(h2_done, m + 1)
                act.activation(h2[:, m, :], psd[m][:, :], ACT.Relu, bias=bt2_sb[:, m:m + 1]).then_inc(h2_ready, 1)
            act.wait_ge(y_done, 1)
            act.activation(y_sb[:, :], psg[0:1, :], ACT.Copy).then_inc(y_ready, 1)

        @block.tensor
        def _(pe):
            def layer0(b, k):
                if k == 0 and not starts(b):
                    pe.wait_ge(x1f_ready, b)
                pe.wait_ge(z0_ready, b * L0T + k + 1)
                if k in SPLIT and not starts(b):
                    i = SPLIT.index(k)
                    pe.wait_ge(z0h_ready, (b - 1) * NS + i + 1)
                    if k == ON_POOL:
                        pe.wait_ge(z0l_pool, b)
                    else:
                        pe.wait_ge(z0l_ready, (b - 1) * (NS - 1) + i)
                    c = slice(COLS * i, COLS * i + COLS)
                    w = slice(M * i, M * i + M)
                    pe.matmul(ps0[:, :], w0h[0:ROWS, w], z0h[0:ROWS, c], start=False, stop=False)
                    pe.matmul(ps0[:, :], w0h[0:ROWS, w], z0l[0:ROWS, c], start=False, stop=False)
                    op = pe.matmul(ps0[:, :], w0l[0:ROWS, w], z0h[0:ROWS, c], start=False, stop=(k == L0_END))
                    if k == L0_END:
                        op.then_inc(l0_done, 1)
                    return
                rows = F * len(range(SPT * k, min(SPT * k + SPT, SHIFTS)))
                op = pe.matmul(ps0[:, :], w0s[0:rows, k, :], pairs[0:rows, k, :], start=(k == 0), stop=(k == L0_END))
                if k == L0_END:
                    op.then_inc(l0_done, 1)

            def turn_x0(b):
                pe.wait_ge(loaded, 16 * LOAD_DMAS * (b + 1))
                if not starts(b):
                    pe.wait_ge(x0c_ready, b * TILES)
                for t in range(TILES):
                    op = pe.transpose(pst[:, ROWS * t:ROWS * t + ROWS], x0t[0:ROWS, 128 * t:128 * t + 128], ident_sb[0:ROWS, :])
                op.then_inc(tr_done, 1)

            def grams(T, t):
                pe.wait_ge(c1_ready, T + 1)
                pe.wait_ge(x0d_ready, T + 1)
                if not isinstance(T, int) or T > 0:
                    pe.wait_ge(g2_copied, T)
                pe.matmul(psg[:, 0:TB * FX], cur1[:, t % 2, :], x0d[:, t % 2, :, :].rearrange("p b f -> p (b f)"),
                          start=True, stop=True).then_inc(g2_done, 1)

            def block_of(b, ahead):
                for t in range(TILES):
                    T = b * TILES + t
                    d, a = D_OFF[t], A_OFF[t]
                    hi, lo = x1h[:, 128 * t:128 * t + 128], x1l[:, 128 * t:128 * t + 128]
                    pe.wait_ge(x1h_ready, T + 1)
                    for g in range(NG):
                        n = M * min(GF, F - GF * g)
                        c = slice(GF * M * g, GF * M * g + n)
                        if PATTERN[t][g] == "d":
                            y, full = psd[d % D_RING], y_d
                            if d >= D_RING or not starts(b):
                                pe.wait_ge(acc_steps, 2 * (b * ND + d - D_RING + 1))
                            d += 1
                        else:
                            y, full = psa[a % A_RING], y_a
                            if a >= A_RING or not starts(b):
                                pe.wait_ge(act_prods, b * NA + a - A_RING + 1)
                            a += 1
                        pe.matmul(y[:, 0:n], hi, w1h[:, c], start=True, stop=False)
                        pe.matmul(y[:, 0:n], hi, w1l[:, c], start=False, stop=False)
                        if g == 0:
                            pe.wait_ge(x1l_ready, T + 1)
                        pe.matmul(y[:, 0:n], lo, w1h[:, c], start=False, stop=True).then_inc(full, 1)
                        if ahead:
                            l0_at = L0_AT_FIRST if starts(b) else L0_AT
                            if (t, g) in l0_at:
                                layer0(b + 1, l0_at[t, g])
                            if t == 1 and g == 5:
                                turn_x0(b + 1)
                        if g == NG - 1 and (t or not starts(b)):
                            grams(T - 1, (t - 1) % TILES)

            pe.wait_ge(w0_summed, 2)
            pe.wait_ge(scr_written, 16 * SCR_DMAS)
            for _ in range(WARMING):
                pe.matmul(ps0[:, :], w0s[0:ROWS, 0, :], w0s[0:ROWS, 0:4, :].rearrange("p t m -> p (t m)"), start=True, stop=True)
            pe.wait_ge(const_in, 16 * 5)
            turn_x0(0)
            for k in [*(k for k in range(L0T) if k != L0_END), L0_END]:
                layer0(0, k)
            pe.wait_ge(w1h_ready, 3)
            pe.wait_ge(w1l_ready, 3)
            pe.wait_ge(w0l_ready, 1)
            block_of(0, True)
            with pe.Fori(1, NBLK - 2) as b:
                block_of(b, True)
            block_of(NBLK - 2, True)
            block_of(NBLK - 1, False)

            pe.wait_ge(mlp_in, 16 * 3)
            pe.wait_ge(x1f_ready, NBLK)
            pe.wait_ge(x0c_ready, NBLK * TILES)
            banks = [ps0, pst, psa[0], psa[1]][:H1T]
            for m, y in enumerate(banks):
                c = slice(128 * m, 128 * m + 128)
                if m == 2:
                    grams(NBLK * TILES - 1, TILES - 1)
                    pe.wait_ge(act_prods, NBLK * NA)
                pe.matmul(y[:, :], wt1_sb[:, 0, c], s0[:, :], start=True, stop=False)
                pe.matmul(y[:, :], wt1_sb[0:16, 3, c], dense_sb, start=False, stop=False)

            pe.wait_ge(g2_copied, NBLK * TILES)
            for f in range(F):
                i = f // W2_CHUNK
                if f == W2_CHUNKS[i][0]:
                    pe.wait_ge(w2h_ready, i + 1)
                    if i == 0:
                        pe.wait_ge(w2l_pool, 1)
                    else:
                        pe.wait_ge(w2l_dve, i)
                m = slice(M * (f % W2_CHUNK), M * (f % W2_CHUNK) + M)
                w_high, w_low = w2_slot(w1h, i)[:, m], w2_slot(w1l, i)[:, m]
                pe.wait_ge(gh_ready, f + 1)
                pe.matmul(psg[:, :], w_high, gram_slot(w1h, f), start=(f == 0), stop=False)
                pe.matmul(psg[:, :], w_low, gram_slot(w1h, f), start=False, stop=False)
                if on_pool(f):
                    pe.wait_ge(gl_pool, turn(f, True))
                else:
                    pe.wait_ge(gl_dve, turn(f, False))
                op = pe.matmul(psg[:, :], w_high, gram_slot(w1l, f), start=False, stop=(f == F - 1))
                op.then_inc(l2_steps, 1)

            for m, y in enumerate(banks):
                c = slice(128 * m, 128 * m + 128)
                pe.matmul(y[:, :], wt1_sb[:, 1, c], gram[:, F, :], start=False, stop=False)
            pe.wait_ge(s2_ready, 1)
            for m, y in enumerate(banks):
                c = slice(128 * m, 128 * m + 128)
                pe.matmul(y[:, :], wt1_sb[:, 2, c], s2[:, :], start=False, stop=True).then_inc(h1_done, 1)
            pe.wait_ge(wt2_in, 16)
            for k in range(H1T):
                pe.wait_ge(h1_ready, k + 1)
                for m in range(H2T):
                    op = pe.matmul(psd[m][:, :], wt2_sb[:, k, 128 * m:128 * m + 128], h1[:, k, :],
                                   start=(k == 0), stop=(k == H1T - 1))
                    if k == H1T - 1:
                        op.then_inc(h2_done, 1)
            for k in range(H2T):
                pe.wait_ge(h2_ready, k + 1)
                op = pe.matmul(psg[0:1, :], wt3_sb[:, k:k + 1], h2[:, k, :], start=(k == 0), stop=(k == H2T - 1))
            op.then_inc(y_done, 1)


def kernel(**inputs):
    import numpy as np
    import concourse.bacc as bacc
    from concourse.bass_utils import run_bass_kernel_spmd

    nc = bacc.Bacc("TRN2", target_bir_lowering=False, num_devices=1)
    arr = {k: np.asarray(v) for k, v in inputs.items()}
    tabs = [arr[f"tbl_{f}"] for f in range(F)]
    start = np.concatenate([[0], np.cumsum([t.shape[0] for t in tabs])])[:F]

    ids = np.concatenate([arr["ids"], arr["ids"][:, 0:CH * FPC - F]], axis=1)
    ids = ids.reshape(NBLK, BB, CH, FPC).transpose(3, 1, 0, 2).reshape(128, NBLK * CH)
    first_row = np.zeros(CH * FPC, np.int32)
    first_row[:F] = start
    base = np.repeat(first_row.reshape(CH, FPC).T, BB, axis=0)

    f_of = np.arange(SPT * L0T * F).reshape(SPT * L0T, F) % F
    g_of = (f_of + np.arange(SPT * L0T)[:, None]) % F
    w0 = arr["L0_rec_f0"]

    def by_tile(rows):
        return np.ascontiguousarray(w0[rows.reshape(-1)].reshape(L0T, ROWS, M).transpose(1, 0, 2))

    samples = np.arange(128)[:, None] // D == np.arange(TB)[None, :]
    arrays = {
        "tables": np.concatenate(tabs, axis=0),
        "ids_and_first_rows": np.ascontiguousarray(np.concatenate([ids, base], axis=1).astype(np.int32)),
        "w0_pairs": by_tile(f_of * F + g_of),
        "w0_mirrored": by_tile(g_of * F + f_of),
        "w1": arr["L0_rec_f1"],
        "w2": arr["L0_rec_f2"],
        "w_top1": arr["W_top1"],
        "b_top1": np.ascontiguousarray(arr["b_top1"].reshape(-1, 128).T),
        "w_top2": arr["W_top2"],
        "b_top2": np.ascontiguousarray(arr["b_top2"].reshape(-1, 128).T),
        "w_top3": np.ascontiguousarray(arr["W_top3"].reshape(-1, 128).T),
        "dense": np.ascontiguousarray(arr["dense_ctx"].T),
        "sample_mask": samples.astype(np.float32),
        "identity": np.eye(ROWS, dtype=np.float32),
    }
    args = [nc.dram_tensor(k, v.shape, mybir.dt.from_np(v.dtype), kind="ExternalInput").ap() for k, v in arrays.items()]
    out = nc.dram_tensor("out_0", (B, 1), F32, kind="ExternalOutput").ap()
    build(nc, *args, out)
    result = run_bass_kernel_spmd(nc, [arrays], core_ids=[0])
    return result.results[0]["out_0"]
```
